# Optimizing a Trainium2 kernel written in Bass

```python
import numpy as np
import jax
import jax.numpy as jnp

def _softmax(x, axis=-1):
    return jax.nn.softmax(x, axis=axis)

def _gelu(x):
    return jax.nn.gelu(x, approximate=True)

def _silu(x):
    return jax.nn.silu(x)

def _sigmoid(x):
    return jax.nn.sigmoid(x)

def _layernorm(x, axis=-1, eps=1e-05):
    m = jnp.mean(x, axis=axis, keepdims=True)
    v = jnp.var(x, axis=axis, keepdims=True)
    return (x - m) / jnp.sqrt(v + eps)

def _scatter_add(tgt, idx, src, axis=0):
    return tgt.at[idx].add(src)

def _segment_sum(src, seg, n):
    return jax.ops.segment_sum(src, seg, n)
kernel_name = 'mk_flamingo_gated_d2_seqx_r8_b7fcfc'

def setup_inputs(seed: int=0):
    np.random.seed(seed)
    _w = jnp.asarray

    def _rec_inputs():
        import jax
        import jax.numpy as jnp
        _rk = jax.random.key(seed)
        x = 6.313e-05 + 0.9998 * jax.random.normal(jax.random.fold_in(_rk, 1), (16, 56, 128), jnp.float32)
        _lenS = 56 - jax.random.randint(jax.random.fold_in(_rk, 7), (16,), 0, max(1, 56 // 4) + 1, jnp.int32)
        _lenS2 = 1500 - jax.random.randint(jax.random.fold_in(_rk, 8), (16,), 0, max(1, 1500 // 4) + 1, jnp.int32)
        _ctx_1024P = jax.random.normal(jax.random.fold_in(_rk, 11), (16, 16, 128), jnp.float32)
        _ctx_1024c = jax.random.dirichlet(jax.random.fold_in(_rk, 511), 0.3 * jnp.ones((16,), jnp.float32), (16, 1500))
        _ctx_1024t = jnp.einsum('bsk,bkd->bsd', _ctx_1024c, _ctx_1024P)
        _ctx_1024t = _ctx_1024t * jax.lax.rsqrt(jnp.mean(jnp.square(_ctx_1024t)) + 1e-12) * 0.953939
        ctx_1024 = -0.000214406 + 1.00034 * (_ctx_1024t + 0.3 * jax.random.normal(jax.random.fold_in(_rk, 611), (16, 1500, 128), jnp.float32))
        _validS = jnp.arange(56)[None, :] < _lenS[:, None]
        _validS2 = jnp.arange(1500)[None, :] < _lenS2[:, None]
        _causal = jnp.tril(jnp.ones((56, 56), dtype=bool))
        mask_1x1xSxS2_bk1 = jnp.broadcast_to(_validS2[0:1, None, None, :], (1, 1, 56, 1500))
        _g = jax.random.normal(jax.random.fold_in(_rk, 9001), (2, 2), jnp.float32)
        _g = jnp.sign(_g) * jnp.maximum(jnp.abs(_g), 1.0) + (_g == 0) * 1.0
        g_xattn = _g[0]
        g_ffn = _g[1]
        return (x, ctx_1024, mask_1x1xSxS2_bk1, g_xattn, g_ffn)
    x, ctx_1024, mask_1x1xSxS2_bk1, g_xattn, g_ffn = _rec_inputs()

    def _L0_xattn_setup():
        import jax, jax.numpy as jnp
        import numpy as np
        from jax import lax
        BIG = jnp.float32(1e+30)

        def _pairwise_euclidean(a, b):
            aa = jnp.sum(a * a, axis=-1)[:, None]
            bb = jnp.sum(b * b, axis=-1)[None, :]
            ab = a @ b.T
            return jnp.sqrt(jnp.maximum(aa + bb - 2.0 * ab, 0.0))

        def _dtw_cost(D):
            row0 = jnp.cumsum(D[0])

            def row_step(prev_row, d_row):
                first = d_row[0] + prev_row[0]

                def col_step(left, inp):
                    d_ij, up, diag = inp
                    r = d_ij + jnp.minimum(jnp.minimum(up, left), diag)
                    return (r, r)
                _, rest = lax.scan(col_step, first, (d_row[1:], prev_row[1:], prev_row[:-1]))
                row = jnp.concatenate([first[None], rest])
                return (row, row)
            _, rows = lax.scan(row_step, row0, D[1:])
            return jnp.concatenate([row0[None], rows], axis=0)

        def _backtrack(R, T1, T2):
            L = T1 + T2 - 1

            def step(carry, _):
                i, j, done = carry
                valid = jnp.logical_not(done)
                cd = jnp.where((i > 0) & (j > 0), R[jnp.maximum(i - 1, 0), jnp.maximum(j - 1, 0)], BIG)
                cu = jnp.where(i > 0, R[jnp.maximum(i - 1, 0), j], BIG)
                cl = jnp.where(j > 0, R[i, jnp.maximum(j - 1, 0)], BIG)
                choice = jnp.argmin(jnp.stack([cd, cu, cl]))
                ni = jnp.where(choice <= 1, i - 1, i)
                nj = jnp.where((choice == 0) | (choice == 2), j - 1, j)
                at_origin = (i == 0) & (j == 0)
                ni = jnp.where(at_origin, 0, ni)
                nj = jnp.where(at_origin, 0, nj)
                return ((ni, nj, done | at_origin), (i, j, valid))
            init = (jnp.int32(T1 - 1), jnp.int32(T2 - 1), jnp.bool_(False))
            _, (i_idx, j_idx, valid) = lax.scan(step, init, None, length=L)
            return (i_idx, j_idx, valid)

        def _align_one(small, large):
            T_small, d = small.shape
            T_large = large.shape[0]
            D = _pairwise_euclidean(small, large)
            R = _dtw_cost(D)
            i_idx, j_idx, valid = _backtrack(R, T_small, T_large)
            contrib = small[i_idx] * valid[:, None].astype(small.dtype)
            expanded = jnp.zeros((T_large, d), dtype=small.dtype).at[j_idx].add(contrib)
            return expanded
        key = jax.random.key(seed)
        k1, k2 = jax.random.split(key)
        teacher = jax.random.normal(k1, (16, 50, 128), dtype=jnp.float32)
        student = jax.random.normal(k2, (16, 75, 128), dtype=jnp.float32)
        return {'teacher_features': teacher, 'student_features': student}
    _L0_xattn_all = _L0_xattn_setup()
    _L0_xattn_in = {k: v for k, v in _L0_xattn_all.items() if k in ()}
    del _L0_xattn_all

    def _L0_ffn_setup():
        import jax, jax.numpy as jnp
        import numpy as np
        B, T, E, C, H, G = (2, 256, 8, 128, 256, 16)
        key = jax.random.key(seed)
        ks = jax.random.split(key, 7)
        return {'hidden_states': jax.random.normal(ks[0], (B, T, C), jnp.float32), 'w_red': jax.random.normal(ks[1], (C, G), jnp.float32) * 0.02, 'wg': jax.random.normal(ks[2], (E, G), jnp.float32), 'W1': jax.random.normal(ks[3], (E, C, H), jnp.float32) * 0.02, 'b1': jax.random.normal(ks[4], (E, H), jnp.float32) * 0.02, 'W2': jax.random.normal(ks[5], (E, H, C), jnp.float32) * 0.02, 'b2': jax.random.normal(ks[6], (E, C), jnp.float32) * 0.02}
    _L0_ffn_all = _L0_ffn_setup()
    _L0_ffn_in = {k: v for k, v in _L0_ffn_all.items() if k in ('w_red', 'wg', 'W1', 'b1', 'W2', 'b2')}
    del _L0_ffn_all

    def _L1_xattn_setup():
        import jax, jax.numpy as jnp
        import numpy as np
        B, S, D, H = (4, 256, 128, 16)
        DK = D // H
        SCALE = 0.02

        def _split_heads(x):
            b, s, _ = x.shape
            return x.reshape(b, s, H, DK).transpose(0, 2, 1, 3)
        key = jax.random.key(seed)
        ks = jax.random.split(key, 12)
        inp = {'q_encodings': jax.random.normal(ks[0], (B, S, D), jnp.float32), 'k_encodings': jax.random.normal(ks[1], (B, S, D), jnp.float32), 'v_encodings': jax.random.normal(ks[2], (B, S, D), jnp.float32), 'mask': jnp.triu(jnp.ones((S, S), jnp.bool_), k=1)[None, None, :, :], 'W_q': jax.random.normal(ks[3], (D, D), jnp.float32) * SCALE, 'b_q': jax.random.normal(ks[4], (D,), jnp.float32) * SCALE, 'W_k': jax.random.normal(ks[5], (D, D), jnp.float32) * SCALE, 'b_k': jax.random.normal(ks[6], (D,), jnp.float32) * SCALE, 'W_v': jax.random.normal(ks[7], (D, D), jnp.float32) * SCALE, 'b_v': jax.random.normal(ks[8], (D,), jnp.float32) * SCALE, 'W_o': jax.random.normal(ks[9], (D, D), jnp.float32) * SCALE, 'b_o': jax.random.normal(ks[10], (D,), jnp.float32) * SCALE}
        return inp
    _L1_xattn_all = _L1_xattn_setup()
    _L1_xattn_in = {k: v for k, v in _L1_xattn_all.items() if k in ('W_q', 'b_q', 'W_k', 'b_k', 'W_v', 'b_v', 'W_o', 'b_o')}
    del _L1_xattn_all

    def _L1_ffn_setup():
        import jax, jax.numpy as jnp
        import numpy as np
        N_EXPERTS = 8
        N_GROUP = 4
        TOPK_GROUP = 2
        TOP_K = 2
        HIDDEN = 128
        INTER = 256
        B, S = (1, 128)

        def _grouped_topk(scores):
            T, E = scores.shape
            per_group = E // N_GROUP
            group_scores = scores.reshape(T, N_GROUP, per_group).max(-1)
            _, gidx = jax.lax.top_k(group_scores, TOPK_GROUP)
            gmask = jnp.zeros((T, N_GROUP), scores.dtype).at[jnp.arange(T)[:, None], gidx].set(1.0)
            smask = jnp.repeat(gmask, per_group, axis=1)
            masked = jnp.where(smask > 0, scores, 0.0)
            topk_w, topk_ids = jax.lax.top_k(masked, TOP_K)
            topk_w = topk_w / topk_w.sum(-1, keepdims=True)
            return (topk_ids, topk_w)
        key = jax.random.key(seed)
        k1, k2, k3, k4 = jax.random.split(key, 4)
        return {'hidden_states': jax.random.normal(k1, (B, S, HIDDEN), jnp.float32), 'gate_w': jax.random.normal(k2, (N_EXPERTS, HIDDEN), jnp.float32) * 0.02, 'w13_weight': jax.random.normal(k3, (N_EXPERTS, 2 * INTER, HIDDEN), jnp.float32) * 0.02, 'w2_weight': jax.random.normal(k4, (N_EXPERTS, HIDDEN, INTER), jnp.float32) * 0.02}
    _L1_ffn_all = _L1_ffn_setup()
    _L1_ffn_in = {k: v for k, v in _L1_ffn_all.items() if k in ('gate_w', 'w13_weight', 'w2_weight')}
    del _L1_ffn_all
    return {'x': x, 'ctx_1024': ctx_1024, 'mask_1x1xSxS2_bk1': mask_1x1xSxS2_bk1, 'g_xattn': g_xattn, 'g_ffn': g_ffn, 'L0_ffn_w_red': _L0_ffn_in['w_red'], 'L0_ffn_wg': _L0_ffn_in['wg'], 'L0_ffn_W1': _L0_ffn_in['W1'], 'L0_ffn_b1': _L0_ffn_in['b1'], 'L0_ffn_W2': _L0_ffn_in['W2'], 'L0_ffn_b2': _L0_ffn_in['b2'], 'L1_xattn_W_q': _L1_xattn_in['W_q'], 'L1_xattn_b_q': _L1_xattn_in['b_q'], 'L1_xattn_W_k': _L1_xattn_in['W_k'], 'L1_xattn_b_k': _L1_xattn_in['b_k'], 'L1_xattn_W_v': _L1_xattn_in['W_v'], 'L1_xattn_b_v': _L1_xattn_in['b_v'], 'L1_xattn_W_o': _L1_xattn_in['W_o'], 'L1_xattn_b_o': _L1_xattn_in['b_o'], 'L1_ffn_gate_w': _L1_ffn_in['gate_w'], 'L1_ffn_w13_weight': _L1_ffn_in['w13_weight'], 'L1_ffn_w2_weight': _L1_ffn_in['w2_weight']}

def reference(x, ctx_1024, mask_1x1xSxS2_bk1, g_xattn, g_ffn, L0_ffn_w_red, L0_ffn_wg, L0_ffn_W1, L0_ffn_b1, L0_ffn_W2, L0_ffn_b2, L1_xattn_W_q, L1_xattn_b_q, L1_xattn_W_k, L1_xattn_b_k, L1_xattn_W_v, L1_xattn_b_v, L1_xattn_W_o, L1_xattn_b_o, L1_ffn_gate_w, L1_ffn_w13_weight, L1_ffn_w2_weight):
    import jax
    import jax.numpy as jnp

    def _L0_xattn_ref(teacher_features, student_features):
        import jax, jax.numpy as jnp
        import numpy as np
        from jax import lax
        BIG = jnp.float32(1e+30)

        def _pairwise_euclidean(a, b):
            aa = jnp.sum(a * a, axis=-1)[:, None]
            bb = jnp.sum(b * b, axis=-1)[None, :]
            ab = a @ b.T
            return jnp.sqrt(jnp.maximum(aa + bb - 2.0 * ab, 0.0))

        def _dtw_cost(D):
            row0 = jnp.cumsum(D[0])

            def row_step(prev_row, d_row):
                first = d_row[0] + prev_row[0]

                def col_step(left, inp):
                    d_ij, up, diag = inp
                    r = d_ij + jnp.minimum(jnp.minimum(up, left), diag)
                    return (r, r)
                _, rest = lax.scan(col_step, first, (d_row[1:], prev_row[1:], prev_row[:-1]))
                row = jnp.concatenate([first[None], rest])
                return (row, row)
            _, rows = lax.scan(row_step, row0, D[1:])
            return jnp.concatenate([row0[None], rows], axis=0)

        def _backtrack(R, T1, T2):
            L = T1 + T2 - 1

            def step(carry, _):
                i, j, done = carry
                valid = jnp.logical_not(done)
                cd = jnp.where((i > 0) & (j > 0), R[jnp.maximum(i - 1, 0), jnp.maximum(j - 1, 0)], BIG)
                cu = jnp.where(i > 0, R[jnp.maximum(i - 1, 0), j], BIG)
                cl = jnp.where(j > 0, R[i, jnp.maximum(j - 1, 0)], BIG)
                choice = jnp.argmin(jnp.stack([cd, cu, cl]))
                ni = jnp.where(choice <= 1, i - 1, i)
                nj = jnp.where((choice == 0) | (choice == 2), j - 1, j)
                at_origin = (i == 0) & (j == 0)
                ni = jnp.where(at_origin, 0, ni)
                nj = jnp.where(at_origin, 0, nj)
                return ((ni, nj, done | at_origin), (i, j, valid))
            init = (jnp.int32(T1 - 1), jnp.int32(T2 - 1), jnp.bool_(False))
            _, (i_idx, j_idx, valid) = lax.scan(step, init, None, length=L)
            return (i_idx, j_idx, valid)

        def _align_one(small, large):
            T_small, d = small.shape
            T_large = large.shape[0]
            D = _pairwise_euclidean(small, large)
            R = _dtw_cost(D)
            i_idx, j_idx, valid = _backtrack(R, T_small, T_large)
            contrib = small[i_idx] * valid[:, None].astype(small.dtype)
            expanded = jnp.zeros((T_large, d), dtype=small.dtype).at[j_idx].add(contrib)
            return expanded
        return jax.vmap(_align_one)(teacher_features, student_features)

    def _L0_ffn_ref(hidden_states, w_red, wg, W1, b1, W2, b2):
        import jax, jax.numpy as jnp
        import numpy as np
        B, T, E, C, H, G = (2, 256, 8, 128, 256, 16)
        b, t, c = hidden_states.shape
        x = hidden_states.reshape(-1, c)
        x_red = x @ w_red
        wg_n = wg / jnp.maximum(jnp.linalg.norm(wg, axis=1, keepdims=True), 0.0001)
        logits = x_red @ wg_n.T
        gates = jax.nn.softmax(logits, axis=1)
        scores = jnp.max(gates, axis=1)
        idx = jnp.argmax(gates, axis=1)
        h = jnp.einsum('nc,ech->neh', x, W1) + b1[None]
        h = jnp.take_along_axis(h, idx[:, None, None], axis=1)[:, 0, :]
        h = jax.nn.gelu(h, approximate=False)
        o = jnp.einsum('nh,ehc->nec', h, W2) + b2[None]
        o = jnp.take_along_axis(o, idx[:, None, None], axis=1)[:, 0, :]
        o = o * scores[:, None]
        return o.reshape(b, t, c)

    def _L1_xattn_ref(q_encodings, k_encodings, v_encodings, mask, W_q, b_q, W_k, b_k, W_v, b_v, W_o, b_o):
        import jax, jax.numpy as jnp
        import numpy as np
        B, S, D, H = (4, 256, 128, 16)
        DK = D // H
        SCALE = 0.02

        def _split_heads(x):
            b, s, _ = x.shape
            return x.reshape(b, s, H, DK).transpose(0, 2, 1, 3)
        q = _split_heads(q_encodings @ W_q + b_q)
        k = _split_heads(k_encodings @ W_k + b_k)
        v = _split_heads(v_encodings @ W_v + b_v)
        scores = jnp.einsum('bhqd,bhkd->bhqk', q, k) / jnp.sqrt(jnp.float32(DK))
        scores = jnp.where(mask, jnp.float32(-1000000000.0), scores)
        attn = jax.nn.softmax(scores, axis=-1)
        ctx = jnp.einsum('bhqk,bhkd->bhqd', attn, v)
        ctx = ctx.transpose(0, 2, 1, 3).reshape(q_encodings.shape[0], -1, D)
        return ctx @ W_o + b_o

    def _L1_ffn_ref(hidden_states, gate_w, w13_weight, w2_weight):
        import jax, jax.numpy as jnp
        import numpy as np
        N_EXPERTS = 8
        N_GROUP = 4
        TOPK_GROUP = 2
        TOP_K = 2
        HIDDEN = 128
        INTER = 256
        B, S = (1, 128)

        def _grouped_topk(scores):
            T, E = scores.shape
            per_group = E // N_GROUP
            group_scores = scores.reshape(T, N_GROUP, per_group).max(-1)
            _, gidx = jax.lax.top_k(group_scores, TOPK_GROUP)
            gmask = jnp.zeros((T, N_GROUP), scores.dtype).at[jnp.arange(T)[:, None], gidx].set(1.0)
            smask = jnp.repeat(gmask, per_group, axis=1)
            masked = jnp.where(smask > 0, scores, 0.0)
            topk_w, topk_ids = jax.lax.top_k(masked, TOP_K)
            topk_w = topk_w / topk_w.sum(-1, keepdims=True)
            return (topk_ids, topk_w)
        Bm, Sm, H = hidden_states.shape
        x = hidden_states.reshape(-1, H)
        T = x.shape[0]
        scores = jax.nn.softmax(x @ gate_w.T, axis=-1)
        topk_ids, topk_w = _grouped_topk(scores)
        combine = jnp.zeros((T, N_EXPERTS), x.dtype).at[jnp.arange(T)[:, None], topk_ids].add(topk_w)
        gu = jnp.einsum('th,eih->tei', x, w13_weight)
        gate, up = (gu[..., :INTER], gu[..., INTER:])
        act = jax.nn.silu(gate) * up
        act = act * combine[:, :, None]
        out = jnp.einsum('tei,ehi->th', act, w2_weight)
        return out.reshape(Bm, Sm, H)
    x = x + jnp.tanh(g_xattn[0]) * _L0_xattn_ref(ctx_1024, _layernorm(x, axis=-1))
    x = x + jnp.tanh(g_ffn[0]) * _L0_ffn_ref(_layernorm(x, axis=-1), L0_ffn_w_red, L0_ffn_wg, L0_ffn_W1, L0_ffn_b1, L0_ffn_W2, L0_ffn_b2)
    x = x + jnp.tanh(g_xattn[1]) * _L1_xattn_ref(_layernorm(x, axis=-1), ctx_1024, ctx_1024, mask_1x1xSxS2_bk1, L1_xattn_W_q, L1_xattn_b_q, L1_xattn_W_k, L1_xattn_b_k, L1_xattn_W_v, L1_xattn_b_v, L1_xattn_W_o, L1_xattn_b_o)
    x = x + jnp.tanh(g_ffn[1]) * _L1_ffn_ref(_layernorm(x, axis=-1), L1_ffn_gate_w, L1_ffn_w13_weight, L1_ffn_w2_weight)
    return x

_drawn_inputs = setup_inputs


def setup_inputs(seed=0):
    import zlib

    import numpy as np

    out = dict(_drawn_inputs(seed))
    spreads = {'g_ffn': (-1.0, 0.6)}
    factors = {'L0_ffn_w_red': 8.0,
     'L0_ffn_wg': 8.0,
     'L0_ffn_W1': 8.0,
     'L0_ffn_b1': 42.405,
     'L0_ffn_W2': 8.0,
     'L0_ffn_b2': 57.938,
     'L1_xattn_W_q': 8.0,
     'L1_xattn_b_q': 34.843,
     'L1_xattn_W_k': 8.0,
     'L1_xattn_W_v': 8.0,
     'L1_xattn_b_v': 33.376,
     'L1_xattn_W_o': 8.0,
     'L1_xattn_b_o': 49.062,
     'L1_ffn_gate_w': 8.0,
     'L1_ffn_w13_weight': 8.0,
     'L1_ffn_w2_weight': 8.0,
     'L1_xattn_b_k': 8.0}
    for name, (base, spread) in spreads.items():
        noise = np.random.default_rng([zlib.crc32(name.encode()), seed]).standard_normal(out[name].shape)
        drawn = base * np.exp(spread * noise) if base else spread * noise
        out[name] = jnp.asarray(drawn.astype(out[name].dtype))
    for name, factor in factors.items():
        out[name] = (out[name] * factor).astype(out[name].dtype)
    return out
```

```python
from contextlib import ExitStack

import numpy as np
import concourse.bass as bass
from concourse import mybir

ALU = mybir.AluOpType
ACT = mybir.ActivationFunctionType
F32 = mybir.dt.float32
I32 = mybir.dt.int32
U8 = mybir.dt.uint8
AX = mybir.AxisListType.X

NB, NQ, ND, NK = 16, 56, 128, 1500
NT = NB // 2
NE = 8
NH, DH = 16, 8
BIG = 1e30
NBLK = 8
BR = -(-NK // NBLK)
LAG = 2
SLOTS = 1 + NQ + LAG * (NBLK - 1)
SW = BR + 1
VG = 3
KC, NC = 125, 12
CH = 500
MAXV = 3e38
EPS = 1e-5
START = 1
ST = NH * NQ // 4


def const_layout():
    names = [("ident", 128), ("shift", 128), ("same", 128), ("ones", 128), ("rows", BR), ("edge", 1),
             ("first", SW), ("sel", 4), ("one4", 4), ("key", NC), ("rank8", 8), ("rank4", 8), ("late", 16), ("blk", NBLK)]
    at, out = 0, {}
    for n, w in names:
        out[n] = (at, w)
        at += w
    return out, at


def const_values():
    lay, width = const_layout()
    c = np.zeros((128, width), np.float32)
    p = np.arange(128)

    def put(name, v):
        a, w = lay[name]
        c[:, a:a + w] = v

    put("ident", np.eye(128))
    put("shift", (p[None, :] == p[:, None] + 16))
    put("same", (p[None, :] % 16 == p[:, None] % 16))
    put("ones", 1.0)
    put("rows", BR * (p[:, None] // 16) + np.arange(BR)[None, :])
    put("edge", np.where(p[:, None] < 16, BIG, 0.0))
    first = np.full((128, SW), BIG)
    first[:16, 0] = 0.0
    put("first", first)
    inh = (p[:, None] % 32) // DH == np.arange(4)[None, :]
    put("sel", inh / np.sqrt(np.float32(DH)))
    put("one4", inh)
    put("key", NC * p[:, None] + np.arange(NC)[None, :])
    put("rank8", NE - np.arange(8))
    put("rank4", np.r_[4 - np.arange(4), np.zeros(4)])
    put("blk", p[:, None] // 16 == np.arange(NBLK)[None, :])
    put("late", np.r_[NC - np.arange(NC), NC, np.zeros(3)])
    return c


SMALL = [("wq", 128), ("wk", 128), ("wv", 128), ("wo", 128), ("wred", 16), ("gate", 8), ("bq", 1), ("bk", 1),
         ("bv", 1), ("b1", 16), ("g", 4)]


def small_layout():
    at, out = 0, {}
    for n, w in SMALL:
        out[n] = (at, w)
        at += w
    return out, at


def flamingo(nc, x, ctx, ctxT, mask, cst_h, small_h, rows_h, wg, w1, w2, w13, w2b, out):
    st = ExitStack()
    clay, cw = const_layout()
    slay, sw = small_layout()
    with st:
        def sb(name, shape, dt=F32):
            return st.enter_context(nc.sbuf_tensor(name, shape, dt))

        def sem(name):
            return st.enter_context(nc.semaphore(name))

        cst = sb("cst", [128, cw])
        small = sb("small", [128, sw])
        rows = sb("rows", [1, NE * 128 + 128])
        wg_s = sb("wg_s", [NE, 16])
        W1 = sb("W1", [128, NE, 256])
        W2 = sb("W2", [128, 2 * NE, 128])
        X = sb("X", [128, NT, 128])
        H = sb("H", [128, NT, 128])
        SQ = sb("SQ", [128, NT, 128])
        HT = sb("HT", [128, NT, 128])
        st8 = sb("st8", [128, 6, NT])
        R = sb("R", [128, SLOTS * SW])
        VM = sb("VM", [128, NC * NB * 64])
        CA = sb("CA", [128, 8 * NC * 128])
        VT = sb("VT", [128, 5, VG * BR])
        mrow = sb("mrow", [128, BR])
        sm = sb("sm", [128, 640])
        live_i = sb("live_i", [1, 4], I32)
        PS = st.enter_context(nc.psum_tensor("PS", [128, 8, 512], F32))

        def C(n):
            a, w = clay[n]
            return cst[:, a:a + w]

        def S(n):
            a, w = slay[n]
            return small[:, a:a + w]

        def small_area(a, w):
            return sm[:, a:a + w]

        Rv = R[:].rearrange("p (t c) -> p t c", c=SW)
        Vcol = VM[:, 0:NQ * BR].rearrange("p (j r) -> p j r", r=BR)
        Mk = VM[:].rearrange("p (c b q) -> p c b q", c=NC, b=NB)
        cT = CA[:, 0:6000].rearrange("p (n k) -> p n k", n=4)
        cSq = CA[:, 6000:9000].rearrange("p (n k) -> p n k", n=2)
        Dt = CA[:, 9000:12000].rearrange("p (n k) -> p n k", n=2)
        nat = [CA[:, 0:8 * NC * 128].rearrange("p (b c d) -> p b c d", b=8, c=NC),
               R[:, 0:8 * NC * 128].rearrange("p (b c d) -> p b c d", b=8, c=NC)]
        gT = CA[:, 0:4096].rearrange("p (n a t) -> p n a t", n=2, a=2)
        sil = CA[:, 4096:6144].rearrange("p (n t) -> p n t", n=2)
        acc = R[:, 0:NB * 2 * ST].rearrange("p (b c) -> p b c", b=NB)
        qbd = R[:, 7168:7168 + NB * 4 * NQ].rearrange("p (b h q) -> p b h q", b=NB, h=4)
        cap = R[:, 10752:12252]
        ckT = CA[:, 0:2000].rearrange("p (b k) -> p b k", b=NB)
        kT = CA[:, 2000:4000].rearrange("p (b k) -> p b k", b=NB)
        vC = CA[:, 4000:6048].rearrange("p (b d) -> p b d", b=NB)
        sS = CA[:, 6048:8048].rearrange("p (g k) -> p g k", g=16)
        pT = CA[:, 8048:8944]
        W13 = VM[:, 0:4096].rearrange("p (e i) -> p e i", e=NE)
        W2B = VM[:, 4096:6144].rearrange("p (e i) -> p e i", e=2 * NE)
        oT = VM[:, 6144:6144 + NB * 64].rearrange("p (b q) -> p b q", b=NB)
        lT = VM[:, 7168:7168 + NB * 64].rearrange("p (b q) -> p b q", b=NB)
        msk8 = VM[:, 8192:8192 + 375].bitcast(U8)
        capA = VM[:, 8700:10200]
        capB = VM[:, 10200:11700]

        tg = small_area(0, 4)
        E = small_area(8, NQ + 1)
        vmax = small_area(72, 1)
        e8 = small_area(76, NBLK)
        wgn = small_area(96, 16)
        wgs = small_area(112, 4)
        wgT = small_area(116, 8)
        lg = small_area(128, 64).rearrange("p (t e) -> p t e", t=NT)
        cf = small_area(192, 64).rearrange("p (t e) -> p t e", t=NT)
        ta = small_area(256, 64).rearrange("p (t e) -> p t e", t=NT)
        tb = small_area(320, 64).rearrange("p (t e) -> p t e", t=NT)
        tc = small_area(384, 64).rearrange("p (t e) -> p t e", t=NT)
        td = small_area(448, 64).rearrange("p (t e) -> p t e", t=NT)
        mx = small_area(512, 64).rearrange("p (u g) -> p u g", u=4)
        mrun = sb("mrun", [128, NT, 16])
        mtmp = sb("mtmp", [128, NT, 16])
        Eb = VT[:].rearrange("p n r -> p (n r)")[:, 0:NB * (NQ + 1)]
        Ed = SQ[:].rearrange("p t d -> p (t d)")[:, 0:NB * (NQ + 1)]
        G1 = H[:].rearrange("p t d -> p (t d)")[:, 0:NB * NQ]
        Ebv = Eb.rearrange("p (b j) -> p b j", b=NB)
        xr = HT[0:16, :, :]
        mk = {"n": 0}

        in_cst = sem("in_cst")
        in_x = sem("in_x")
        in_w = sem("in_w")
        in_ct = [sem(f"in_ct{i}") for i in range(4)]
        in_nat = sem("in_nat")
        in_nat2 = sem("in_nat2")
        in_w13 = sem("in_w13")
        in_mask = sem("in_mask")
        vec = sem("vec_step")
        pool_init = sem("pool_init")
        ln_var = sem("ln_var")
        ln_std = sem("ln_std")
        ln_out = sem("ln_out")
        ht_ps = sem("ht_ps")
        ht_sb = sem("ht_sb")
        sq_ok = sem("ctx_squared")
        d_ps = sem("dist_psum")
        d_add = sem("dist_added")
        d_root = sem("dist_root")
        d_put = [sem(f"dist_placed{i}") for i in range(2)]
        w_min = sem("wave_min")
        w_row = sem("wave_row")
        w_shift = sem("wave_shifted")
        w_edge = sem("wave_edge")
        v_grp = sem("choice_group")
        v_put = [sem(f"choice_placed{i}") for i in range(2)]
        b_g = sem("back_mask")
        b_max = sem("back_blockmax")
        b_t = sem("back_transposed")
        b_e = sem("back_max")
        b_bc = sem("back_threshold")
        e_tab = sem("e_diag")
        e_bc = sem("e_broadcast")
        m_ok = sem("path_mask")
        x_ps = sem("aligned_psum")
        x_up = sem("x_updated")
        wg_t = sem("router_transposed")
        wg_r = sem("router_ready")
        wg_sq = sem("router_squares")
        wg_std = sem("router_norms")
        lg_ps = sem("logits_psum")
        lg_rd = sem("router_reduced")
        r_max = sem("route_max")
        r_exp = sem("route_exp")
        h_ps = sem("hidden_psum")
        h_act = sem("hidden_act")
        h_mul = sem("hidden_mul")
        o_ps = sem("expert_psum")
        o_add = sem("expert_added")
        tanh_ok = sem("gates_tanh")
        q_ps = sem("query_psum")
        q_sb = sem("query_blocks")
        cap_ok = sem("mask_cap")
        c0_t = sem("first_chunk_psum")
        c0_f = sem("first_chunk_flags")
        c0_ok = sem("first_chunk")
        a_in = sem("attn_ctx_in")
        a_kps = sem("attn_k_psum")
        a_kT = sem("attn_k")
        a_vps = sem("attn_v_psum")
        a_v = sem("attn_v")
        a_s = sem("attn_scores")
        a_min = sem("attn_capped")
        a_max = sem("attn_max")
        a_sub = sem("attn_shifted")
        a_exp = sem("attn_exp")
        a_tp = sem("attn_p_transposed")
        a_pT = sem("attn_pT")
        a_o = sem("attn_out_psum")
        a_acc = sem("attn_accumulated")
        a_end = sem("attn_rows")
        a_fin = sem("attn_norm")
        wo_ps = sem("attn_projected")
        out_s = sem("out_stored")

        block = st.enter_context(nc.Block())
        NLN = 4
        def placed(g):
            t0, t1 = 1 + VG * g, min(1 + VG * (g + 1), SLOTS)
            for k in range(NBLK):
                a = max(t0, 2 + LAG * k)
                b = min(t1, NQ + 1 + LAG * k)
                if a < b:
                    yield k, a - t0, b - a, a - 1 - LAG * k
        NG = -(-(SLOTS - 1) // VG)
        put_count = [sum(1 for _ in placed(g)) for g in range(NG)]

        @block.sync
        def _(sp):
            sp.dma_start(cst[:], cst_h).then_inc(in_cst, 16)
            xs = x.rearrange("(t h) q d -> h q t d", h=2)
            sp.wait_ge(pool_init, 1)
            sp.dma_start(X[0:NQ, :, :], xs[0]).then_inc(in_x, 16)
            sp.dma_start(X[64:64 + NQ, :, :], xs[1]).then_inc(in_x, 16)
            sp.dma_start(small[:], small_h).then_inc(in_cst, 16)
            for b in range(4):
                sp.dma_start(cT[:, b, :], ctxT[b]).then_inc(in_ct[b], 16)
            sp.dma_start(rows[:], rows_h).then_inc(in_w, 16)
            sp.dma_start(wg_s[:], wg).then_inc(in_w, 16)
            sp.dma_start(W1[:], w1.rearrange("e c h -> c e h")).then_inc(in_w, 16)
            sp.dma_start(W2[:], w2).then_inc(in_w, 16)
            for u in range(NT):
                sp.wait_ge(d_root, u + 1)
                if u == 0:
                    sp.wait_ge(pool_init, 2)
                for k in range(NBLK):
                    n = min(BR, NK - BR * k)
                    for h in range(2):
                        p = 16 * k + 2 * u + h
                        sp.dma_start(Rv[p:p + 1, 1 + LAG * k:1 + LAG * k + NQ, 1:1 + n],
                                     Dt[64 * h:64 * h + NQ, u % 2, BR * k:BR * k + n]).then_inc(d_put[u % 2], 16)
                for b in (2 * u + 4, 2 * u + 5):
                    if b < NB:
                        sp.wait_ge(d_ps, u + 1)
                        sp.dma_start(cT[:, b % 4, :], ctxT[b]).then_inc(in_ct[b % 4], 16)
            for i in range(2):
                sp.wait_ge(d_put[i], 16 * 16 * NT // 2)
            sp.dma_start(nat[0][0:KC], ctx.rearrange("b (p c) d -> p b c d", c=NC)[:, 0:8]).then_inc(in_nat, 16)
            for g in range(NG):
                sp.wait_ge(v_grp, g + 1)
                for k, a, n, j in placed(g):
                    sp.dma_start(Vcol[16 * k:16 * k + 16, j:j + n, :],
                                 VT[16 * k:16 * k + 16, 3 + g % 2, a * BR:(a + n) * BR].rearrange(
                                     "p (j r) -> p j r", r=BR)).then_inc(v_put[g % 2], 16)
            sp.dma_start(nat[1][0:KC], ctx.rearrange("b (p c) d -> p b c d", c=NC)[:, 8:16]).then_inc(in_nat2, 16)
            sp.wait_ge(x_ps, 1)
            sp.dma_start(W13, w13).then_inc(in_w13, 16)
            sp.dma_start(W2B, w2b).then_inc(in_w13, 16)
            for h in range(2):
                sp.dma_start(msk8[NQ * h:NQ * h + NQ, :], mask).then_inc(in_mask, 16)
            sp.wait_ge(o_add, NE)
            sp.wait_ge(c0_ok, 1)
            live = sp.value_load(live_i[0:1, 0:1], min_val=1, max_val=NC)
            for ph in range(2):
                with sp.Fori(0, live) as n:
                    m = n + live if ph else n
                    key = sp.snap(n * -KC + (NC - 1) * KC)
                    sp.wait_ge(a_vps, 4 * m + START)
                    sp.dma_start(ckT, ctxT.rearrange("b d k -> d b k")[:, :, bass.ds(key, KC)]).then_inc(a_in, 16)
            sp.wait_ge(o_add, 2 * NE)
            os = out.rearrange("(t h) q d -> h q t d", h=2)
            sp.dma_start(os[0], X[0:NQ, :, :]).then_inc(out_s, 16)
            sp.dma_start(os[1], X[64:64 + NQ, :, :]).then_inc(out_s, 16)
            sp.wait_ge(out_s, 32)

        @block.gpsimd
        def _(pool):
            for s in (a_min, a_max, a_tp, a_acc, a_o, a_pT, a_vps):
                pool.sem_inc(s, START)
            pool.memset(X[:], 0.0).then_inc(pool_init, 1)
            pool.memset(R[:], BIG).then_inc(pool_init, 1)
            pool.memset(VM[:], 0.0).then_inc(pool_init, 1)

        @block.tensor
        def _(pe):
            ident = C("ident")

            def transposes(n):
                pe.wait_ge(ln_out, n + 1)
                if n == 1:
                    pe.wait_ge(x_up, 1)
                for t in range(NT):
                    last = pe.transpose(PS[:, 6 + t // 4, 128 * (t % 4):128 * (t % 4) + 128], H[:, t, :], ident)
                last.then_inc(ht_ps, 1)

            pe.wait_ge(in_cst, 32)
            transposes(0)
            pe.wait_ge(ht_sb, 2)
            for u in range(NT):
                if u >= 2:
                    pe.wait_ge(d_add, u - 1)
                if u == 1:
                    pe.wait_ge(d_add, 1)
                for h in range(2):
                    b = 2 * u + h
                    pe.wait_ge(sq_ok, b + 1)
                    pe.wait_ge(in_ct[b % 4], 16 * (b // 4 + 1))
                    for i in range(3):
                        o = PS[64 * h:64 * h + 64, 3 * (u % 2) + i, 0:CH]
                        pe.matmul(o, C("ones")[:, 0:64], cSq[:, h, CH * i:CH * i + CH], start=True, stop=False)
                        last = pe.matmul(o, HT[:, u, 64 * h:64 * h + 64], cT[:, b % 4, CH * i:CH * i + CH],
                                         start=False, stop=True)
                last.then_inc(d_ps, 1)
            pe.wait_ge(d_add, NT)
            pe.wait_ge(w_row, 1)
            pe.matmul(PS[:, 0, 0:1], C("shift"), Rv[:, 0, BR:BR + 1], start=True, stop=True).then_inc(w_shift, 1)
            with pe.Fori(1, SLOTS - 2) as t:
                pe.wait_ge(w_row, t + 1)
                pe.wait_ge(w_edge, t)
                pe.matmul(PS[:, 0, bass.ds(t, 1)], C("shift"), Rv[:, bass.ds(t, 1), BR:BR + 1].rearrange(
                    "p a b -> p (a b)"), start=True, stop=True).then_inc(w_shift, 1)
            with pe.Fori(0, NQ - 1) as n:
                pe.wait_ge(b_t, n + 1)
                pe.matmul(PS[:, 1, bass.ds(n * NBLK, NBLK)], C("same"), e8, start=True, stop=True).then_inc(b_bc, 1)
            pe.wait_ge(e_tab, 1)
            W = NB * (NQ + 1) // 2
            for i in range(2):
                last = pe.matmul(PS[:, 3 + i, 0:W], C("ones")[0:16, :], Ed[0:16, W * i:W * i + W],
                                 start=True, stop=True)
            last.then_inc(e_bc, 1)
            pe.wait_ge(m_ok, NC)
            pe.wait_ge(in_nat, 16)
            for b in range(NB):
                if b == 8:
                    pe.wait_ge(in_nat2, 16)
                for c in range(NC):
                    last = pe.matmul(PS[64 * (b % 2):64 * (b % 2) + 64, 5 + (b // 8), 128 * (b // 2 % 4):128 * (b // 2 % 4) + 128],
                                     Mk[0:KC, c, b, :], nat[b // 8][0:KC, b % 8, c, :],
                                     start=(c == 0), stop=(c == NC - 1))
            last.then_inc(x_ps, 1)

            def hidden(e, w, half_of):
                for a, (wt, bank) in enumerate(half_of):
                    for t in range(2):
                        last = pe.matmul(PS[:, bank + t, :], wt, HT[:, 4 * t:4 * t + 4, :], start=True, stop=True)
                return last

            def experts_out(e, w, bias, g):
                for t in range(NT):
                    o = PS[:, 4 + t // 4, 128 * (t % 4):128 * (t % 4) + 128]
                    for a in range(2):
                        last = pe.matmul(o, g[:, a, 128 * t:128 * t + 128], w[:, 2 * e + a, :],
                                         start=(a == 0), stop=(a == 1 and not bias))
                    if bias:
                        last = pe.matmul(o, C("ones")[0:1, :], rows[0:1, 128 * e:128 * e + 128],
                                         start=False, stop=True)
                return last

            pe.wait_ge(in_w, 64)
            pe.wait_ge(wg_r, 1)
            pe.transpose(PS[0:16, 3, 0:8], wgn[0:8, :], C("ident")[0:8, 0:8]).then_inc(wg_t, 1)
            transposes(1)
            pe.wait_ge(ht_sb, 3)
            for t in range(2):
                last = pe.matmul(PS[0:16, t, :], S("wred"), HT[:, 4 * t:4 * t + 4, :], start=True, stop=True)
            last.then_inc(lg_ps, 1)
            pe.wait_ge(lg_rd, 2)
            for t in range(NT):
                last = pe.matmul(PS[:, 3, 64 + 8 * t:72 + 8 * t], SQ[0:16, t, :], wgT[0:16, :], start=True, stop=True)
            last.then_inc(lg_ps, 1)
            pe.wait_ge(r_max, 1)
            for e in range(NE):
                if e:
                    pe.wait_ge(h_act, 2 * e)
                hidden(e, W1, [(W1[:, e, 0:128], 0), (W1[:, e, 128:256], 2)]).then_inc(h_ps, 1)
                pe.wait_ge(h_act, 2 * e + 2)
                if e:
                    pe.wait_ge(o_add, e)
                else:
                    pe.wait_ge(x_up, 1)
                experts_out(e, W2, True, gT[:, e % 2]).then_inc(o_ps, 1)

            pe.wait_ge(cap_ok, 1)
            pe.transpose(PS[0:13, 0, 0:56], sm[0:56, 576:589], C("ident")[0:56, 0:56]).then_inc(c0_t, 1)
            pe.wait_ge(c0_f, 1)
            pe.transpose(PS[0:1, 0, 64:77], sm[0:13, 592:593], C("ident")[0:13, 0:13]).then_inc(c0_t, 1)
            pe.wait_ge(c0_ok, 1)
            transposes(2)
            pe.wait_ge(ht_sb, 4)
            for t in range(2):
                last = pe.matmul(PS[:, t, :], S("wq"), HT[:, 4 * t:4 * t + 4, :], start=True, stop=True)
            last.then_inc(q_ps, 1)
            pe.wait_ge(q_sb, 1)
            pe.wait_ge(c0_ok, 1)
            live = pe.value_load(live_i[0:1, 0:1], min_val=1, max_val=NC)

            def project(n):
                pe.wait_ge(a_in, 16 * n + 16)
                pe.wait_ge(a_min, NT * n + START)
                for i in range(4):
                    last = pe.matmul(PS[:, i, 0:CH], S("wk"), ckT[:, 4 * i:4 * i + 4, :], start=True, stop=True)
                last.then_inc(a_kps, 1)
                for i in range(4):
                    pe.wait_ge(a_kT, 4 * n + i + 1)
                    for b in range(4):
                        last = pe.matmul(PS[0:KC, i, 128 * b:128 * b + 128], ckT[:, 4 * i + b, :], S("wv"),
                                         start=True, stop=True)
                    last.then_inc(a_vps, 1)

            def scores(n, u):
                pe.wait_ge(a_v, 4 * n + 4)
                pe.wait_ge(a_min, NT * n + u + START)
                for h in range(2):
                    b = 2 * u + h
                    for g in range(4):
                        for pr in range(2):
                            k = 2 * h + pr
                            last = pe.matmul(PS[0:112, g, KC * k:KC * k + KC],
                                             qbd[32 * g:32 * g + 32, b, 2 * pr:2 * pr + 2, :],
                                             kT[32 * g:32 * g + 32, b, :], start=True, stop=True,
                                             tile_position=(32 * g, 0))
                last.then_inc(a_s, 1)

            with pe.Fori(0, live) as n:
                project(n)
                for u in range(NT):
                    scores(n, u)
            with pe.Fori(0, live) as n:
                m = n + live
                project(m)
                for u in range(NT):
                    scores(m, u)
                    pe.wait_ge(a_exp, NT * n + u + 1)
                    for h in range(2):
                        b = 2 * u + h
                        pe.wait_ge(a_pT, 16 * n + b + START)
                        for g in range(4):
                            for pr in range(2):
                                last = pe.transpose(PS[0:KC, 4 + g // 2, 224 * (g % 2) + 112 * pr:224 * (g % 2) + 112 * pr + 112],
                                                    sS[0:112, 4 * g + 2 * h + pr, :], C("ident")[0:112, 0:112])
                        last.then_inc(a_tp, 1)
                        pe.wait_ge(a_pT, 16 * n + b + 1 + START)
                        pe.wait_ge(a_acc, 16 * n + b + START)
                        for g in range(4):
                            pe.matmul(PS[32 * g:32 * g + 32, 6, 0:ST], vC[0:KC, b, 32 * g:32 * g + 32],
                                      pT[0:KC, ST * g:ST * g + ST], start=True, stop=True, tile_position=(0, 32 * g))
                            last = pe.matmul(PS[32 * g:32 * g + 32, 6, ST:2 * ST], C("ones")[0:KC, 0:32],
                                             pT[0:KC, ST * g:ST * g + ST], start=True, stop=True,
                                             tile_position=(0, 32 * g))
                        last.then_inc(a_o, 1)
            pe.wait_ge(a_fin, 1)
            for t in range(NT):
                o = PS[:, t // 4, 128 * (t % 4):128 * (t % 4) + 128]
                pe.matmul(o, oT[:, 2 * t:2 * t + 2, :], S("wo"), start=True, stop=False)
                last = pe.matmul(o, C("ones")[0:1, :], rows[0:1, 1024:1152], start=False, stop=True)
            last.then_inc(wo_ps, 1)

            pe.wait_ge(in_w13, 32)
            transposes(3)
            pe.wait_ge(ht_sb, 5)
            for t in range(NT):
                last = pe.matmul(PS[:, 3, 64 + 8 * t:72 + 8 * t], HT[:, t, :], S("gate"), start=True, stop=True)
            last.then_inc(lg_ps, 1)
            pe.wait_ge(r_max, 2)
            for e in range(NE):
                for a in range(2):
                    if e or a:
                        pe.wait_ge(h_mul, 2 * e + a)
                    hidden(e, W13, [(W13[:, e, 128 * a:128 * a + 128], 0),
                                    (W13[:, e, 256 + 128 * a:384 + 128 * a], 2)]).then_inc(h_ps, 1)
                pe.wait_ge(h_mul, 2 * e + 2)
                pe.wait_ge(o_add, NE + e)
                experts_out(e, W2B, False, gT[:, e % 2]).then_inc(o_ps, 1)

        @block.scalar
        def _(act):
            act.wait_ge(in_cst, 32)
            act.activation(tg, S("g"), ACT.Tanh).then_inc(tanh_ok, 1)

            def root(n):
                act.wait_ge(ln_var, n)
                act.activation(st8[:, 3, :], st8[:, 2, :], ACT.Sqrt).then_inc(ln_std, 1)

            def copy_ht(n, scale):
                act.wait_ge(ht_ps, n)
                act.activation(HT[:], PS[:, 6:8, :].rearrange("p a (t d) -> p (a t) d", d=128), ACT.Copy,
                               scale=scale).then_inc(ht_sb, 2 if n == 1 else 1)

            root(1)
            copy_ht(1, -2.0)
            for b in range(NB):
                u = b // 2
                act.wait_ge(in_ct[b % 4], 16 * (b // 4 + 1))
                if b >= 2:
                    act.wait_ge(d_ps, u)
                act.activation(cSq[:, b % 2, :], cT[:, b % 4, :], ACT.Square).then_inc(sq_ok, 1)
                if b % 2 == 0 and u:
                    act.wait_ge(d_add, u)
                    act.activation(Dt[:, (u - 1) % 2, :], Dt[:, (u - 1) % 2, :], ACT.Sqrt).then_inc(d_root, 1)
            act.wait_ge(d_add, NT)
            act.activation(Dt[:, (NT - 1) % 2, :], Dt[:, (NT - 1) % 2, :], ACT.Sqrt).then_inc(d_root, 1)
            with act.Fori(0, SLOTS - 2) as t:
                act.wait_ge(w_shift, t + 1)
                act.activation(Rv[:, bass.ds(t + 2, 1), 0:1].rearrange("p a b -> p (a b)"), PS[:, 0, bass.ds(t, 1)],
                               ACT.Identity, bias=C("edge")).then_inc(w_edge, 1)
            act.wait_ge(wg_sq, 1)
            act.activation(wgs[0:8, 1:2], wgs[0:8, 0:1], ACT.Sqrt).then_inc(wg_std, 1)
            act.wait_ge(wg_t, 1)
            act.activation(wgT[0:16, :], PS[0:16, 3, 0:8], ACT.Copy).then_inc(lg_rd, 1)
            root(2)
            copy_ht(2, 1.0)
            act.wait_ge(lg_ps, 1)
            act.activation(SQ[0:16, :, :], PS[0:16, 0:2, :].rearrange("p a (t d) -> p (a t) d", d=128),
                           ACT.Copy).then_inc(lg_rd, 1)
            act.wait_ge(r_exp, 1)
            act.activation(ta, lg, ACT.Exp).then_inc(r_exp, 1)
            for e in range(NE):
                act.wait_ge(h_ps, e + 1)
                for a in range(2):
                    if e >= 2:
                        act.wait_ge(o_ps, e - 1)
                    act.activation(gT[:, e % 2, a, :], PS[:, 2 * a:2 * a + 2, :].rearrange("p a t -> p (a t)"), ACT.Gelu,
                                   bias=S("b1")[:, 2 * e + a:2 * e + a + 1]).then_inc(h_act, 1)
            root(3)
            copy_ht(3, 1.0)
            act.wait_ge(c0_ok, 1)
            live = act.value_load(live_i[0:1, 0:1], min_val=1, max_val=NC)

            def keys(n):
                for i in range(4):
                    act.wait_ge(a_kps, n + 1)
                    act.activation(kT[:, 4 * i:4 * i + 4, :], PS[:, i, 0:CH].rearrange("p (b k) -> p b k", b=4),
                                   ACT.Identity, bias=S("bk")).then_inc(a_kT, 1)
                for i in range(4):
                    act.wait_ge(a_vps, 4 * n + i + 1 + START)
                    act.activation(vC[0:KC, 4 * i:4 * i + 4, :], PS[0:KC, i, :].rearrange("p (b d) -> p b d", b=4),
                                   ACT.Copy).then_inc(a_v, 1)

            with act.Fori(0, live) as n:
                keys(n)
            with act.Fori(0, live) as n:
                keys(n + live)
                for u in range(NT):
                    act.wait_ge(a_sub, NT * n + u + 1)
                    act.activation(sS[0:112], sS[0:112], ACT.Exp).then_inc(a_exp, 1)
                    for h in range(2):
                        b = 2 * u + h
                        act.wait_ge(a_tp, 16 * n + b + 1 + START)
                        act.wait_ge(a_o, 16 * n + b + START)
                        act.activation(pT[0:KC, :], PS[0:KC, 4:6, 0:448], ACT.Copy).then_inc(a_pT, 1)
            root(4)
            copy_ht(4, 1.0)
            act.wait_ge(r_exp, 3)
            act.activation(ta, lg, ACT.Exp).then_inc(r_exp, 1)
            for e in range(NE):
                for a in range(2):
                    n = 2 * e + a
                    act.wait_ge(h_ps, NE + n + 1)
                    if n >= 2:
                        act.wait_ge(h_mul, n - 1)
                    act.activation(sil[:, a, :], PS[:, 0:2, :].rearrange("p a t -> p (a t)"), ACT.Silu).then_inc(h_act, 1)

        @block.vector
        def _(dve):
            n_vec = [0]

            def link(ins):
                n_vec[0] += 1
                ins.then_inc(vec, 1)
                dve.wait_ge(vec, n_vec[0])

            s8 = [st8[:, i, :] for i in range(6)]

            def bc(a):
                return a[:, :, None].to_broadcast([128, NT, 128])

            def layernorm(n):
                link(dve.tensor_reduce(s8[0], X[:], AX, ALU.add))
                link(dve.tensor_scalar(s8[1], s8[0], -1.0 / ND, None, ALU.mult))
                link(dve.tensor_tensor(H[:], X[:], bc(s8[1]), ALU.add))
                link(dve.tensor_tensor(SQ[:], H[:], H[:], ALU.mult))
                link(dve.tensor_reduce(s8[0], SQ[:], AX, ALU.add))
                dve.tensor_scalar(s8[2], s8[0], 1.0 / ND, EPS, ALU.mult, ALU.add).then_inc(ln_var, 1)
                dve.wait_ge(ln_std, n)
                link(dve.reciprocal(s8[4], s8[3]))
                dve.tensor_tensor(H[:], H[:], bc(s8[4]), ALU.mult).then_inc(ln_out, 1)

            dve.wait_ge(in_cst, 32)
            dve.wait_ge(in_x, 32)
            dve.wait_ge(pool_init, 2)
            link(dve.tensor_copy(Rv[:, 0, :], C("first")))
            dve.tensor_scalar(mrow[:, 0:1], C("rows")[:, 0:1], 1.0, None, ALU.mult).then_inc(w_row, 1)
            layernorm(1)
            dve.wait_ge(ln_out, 1)
            link(dve.tensor_tensor(SQ[:], H[:], H[:], ALU.mult))
            link(dve.tensor_reduce(s8[5], SQ[:], AX, ALU.add))
            for u in range(NT):
                dve.wait_ge(d_ps, u + 1)
                if u >= 2:
                    dve.wait_ge(d_put[u % 2], 16 * 16 * (u // 2))
                dve.tensor_scalar(Dt[:, u % 2, :].rearrange("p (i k) -> p i k", i=3),
                                  PS[:, 3 * (u % 2):3 * (u % 2) + 3, 0:CH], s8[5][:, u:u + 1], 0.0,
                                  ALU.add, ALU.max).then_inc(d_add, 1)
            for i in range(2):
                dve.wait_ge(d_put[i], 16 * 16 * NT // 2)

            def wave(t):
                dve.tensor_tensor(mrow[:], Rv[:, bass.ds(t - 1, 1), 1:SW].rearrange("p a b -> p (a b)"),
                                  Rv[:, bass.ds(t - 1, 1), 0:BR].rearrange("p a b -> p (a b)"), ALU.min).then_inc(w_min, 1)
                dve.wait_ge(w_min, t)
                row = Rv[:, bass.ds(t, 1), 1:SW].rearrange("p a b -> p (a b)")
                return row

            row = wave(1)
            dve.tensor_tensor_scan(row, mrow[:], row, Rv[:, 1, 0:1], ALU.min, ALU.add).then_inc(w_row, 1)
            with dve.Fori(2, SLOTS) as t:
                dve.wait_ge(w_row, t)
                row = wave(t)
                dve.wait_ge(w_edge, t - 1)
                dve.tensor_tensor_scan(row, mrow[:], row, Rv[:, bass.ds(t, 1), 0:1].rearrange("p a b -> p (a b)"),
                                       ALU.min, ALU.add).then_inc(w_row, 1)
            dve.wait_ge(w_row, SLOTS)
            dve.wait_ge(pool_init, 3)

            for g in range(NG):
                t0, t1 = 1 + VG * g, min(1 + VG * (g + 1), SLOTS)
                n = t1 - t0
                f = [VT[:, i, 0:n * BR].rearrange("p (t r) -> p t r", r=BR) for i in range(5)]
                cl, cd, cu = Rv[:, t0 - 1:t1 - 1, 1:SW], Rv[:, t0 - 1:t1 - 1, 0:BR], Rv[:, t0:t1, 0:BR]
                w = C("rows")[:, None, :].to_broadcast([128, n, BR])
                dve.tensor_tensor(f[0], cu, cd, ALU.is_lt)
                link(dve.tensor_tensor(f[1], cu, cl, ALU.is_le))
                link(dve.tensor_tensor(f[0], f[0], f[1], ALU.mult))
                link(dve.tensor_tensor(f[1], cd, cl, ALU.is_le))
                link(dve.scalar_tensor_tensor(f[1], f[1], -0.5, w, ALU.mult, ALU.add))
                if g >= 2:
                    dve.wait_ge(v_put[g % 2], 16 * sum(put_count[g % 2:g:2]))
                dve.scalar_tensor_tensor(f[3 + g % 2], f[0], 0.5, f[1], ALU.is_lt, ALU.mult).then_inc(v_grp, 1)
                dve.wait_ge(v_grp, g + 1)
            for i in range(2):
                dve.wait_ge(v_put[i], 16 * sum(put_count[i::2]))

            dve.memset(E[:, 0:1], 0.0)
            link(dve.memset(E[:, NQ:NQ + 1], float(NK - 1)))
            for n in range(NQ - 1):
                if n:
                    dve.wait_ge(b_e, n)
                dve.tensor_scalar(mrow[:], C("rows"), E[:, NQ - n:NQ - n + 1], None, ALU.is_le).then_inc(b_g, 1)
                dve.wait_ge(b_g, n + 1)
                dve.tensor_tensor_reduce(mrow[:], mrow[:], Vcol[:, NQ - 1 - n, :],
                                         1.0, 0.0, ALU.mult, ALU.max, vmax).then_inc(b_max, 1)
                dve.wait_ge(b_max, n + 1)
                dve.tensor_scalar(e8, C("blk"), vmax, None, ALU.mult).then_inc(b_t, 1)
                dve.wait_ge(b_bc, n + 1)
                dve.tensor_reduce(E[:, NQ - 1 - n:NQ - n], PS[:, 1, n * NBLK:(n + 1) * NBLK], AX, ALU.max).then_inc(b_e, 1)
            dve.wait_ge(b_e, NQ - 1)
            dve.tensor_tensor(Ed[0:16, :].rearrange("p (b j) -> p b j", b=NB),
                              E[0:16, None, :].to_broadcast([16, NB, NQ + 1]),
                              C("ident")[0:16, 0:16, None].to_broadcast([16, NB, NQ + 1]), ALU.mult).then_inc(e_tab, 1)
            dve.wait_ge(e_bc, 1)
            W = NB * (NQ + 1) // 2
            link(dve.tensor_copy(Eb.rearrange("p (i w) -> p i w", i=2), PS[:, 3:5, 0:W]))
            link(dve.memset(VM[:], 0.0))
            G1v = G1.rearrange("p (b q) -> p b q", b=NB)
            for c in range(NC):
                i = C("key")[:, c:c + 1]
                link(dve.tensor_scalar(G1v, Ebv[:, :, 1:NQ + 1], i, None, ALU.is_ge))
                dve.scalar_tensor_tensor(Mk[:, c, :, 0:NQ], Ebv[:, :, 0:NQ], i, G1v, ALU.is_le, ALU.mult).then_inc(m_ok, 1)
                dve.wait_ge(m_ok, c + 1)
            dve.wait_ge(tanh_ok, 1)
            dve.wait_ge(in_w, 64)
            link(dve.tensor_tensor(wgn[0:8, :], wg_s[:], wg_s[:], ALU.mult))
            dve.tensor_reduce(wgs[0:8, 0:1], wgn[0:8, :], AX, ALU.add).then_inc(wg_sq, 1)
            dve.wait_ge(wg_std, 1)
            link(dve.tensor_scalar(wgs[0:8, 2:3], wgs[0:8, 1:2], 1e-4, None, ALU.max))
            link(dve.reciprocal(wgs[0:8, 3:4], wgs[0:8, 2:3]))
            dve.tensor_scalar(wgn[0:8, :], wg_s[:], wgs[0:8, 3:4], None, ALU.mult).then_inc(wg_r, 1)
            dve.wait_ge(x_ps, 1)
            dve.scalar_tensor_tensor(X[:].rearrange("p t d -> p (t d)").rearrange("p (a w) -> p a w", a=2), PS[:, 5:7, :],
                                     tg[:, 0:1], X[:].rearrange("p t d -> p (t d)").rearrange("p (a w) -> p a w", a=2),
                                     ALU.mult, ALU.add).then_inc(x_up, 1)
            dve.wait_ge(x_up, 1)

            def softmax(n):
                link(dve.tensor_copy(lg, PS[:, 3, 64:128].rearrange("p (t e) -> p t e", t=NT)))
                link(dve.tensor_reduce(s8[0], lg, AX, ALU.max))
                dve.tensor_tensor(lg, lg, s8[0][:, :, None].to_broadcast([128, NT, NE]), ALU.subtract).then_inc(r_exp, 1)
                dve.wait_ge(r_exp, n)
                link(dve.tensor_reduce(s8[0], ta, AX, ALU.add))
                link(dve.reciprocal(s8[1], s8[0]))
                link(dve.tensor_tensor(ta, ta, s8[1][:, :, None].to_broadcast([128, NT, NE]), ALU.mult))

            def first_of(dst, src, w, m):
                tmp = td[:, :, 0:w]
                rank = C("rank8" if w == 8 else "rank4")[:, None, 0:w].to_broadcast([128, NT, w])
                link(dve.tensor_reduce(m, src, AX, ALU.max))
                link(dve.tensor_tensor(dst, src, m[:, :, None].to_broadcast([128, NT, w]), ALU.is_equal))
                link(dve.tensor_tensor(dst, dst, rank, ALU.mult))
                link(dve.tensor_reduce(s8[5], dst, AX, ALU.max))
                link(dve.tensor_tensor(dst, dst, s8[5][:, :, None].to_broadcast([128, NT, w]), ALU.is_equal))

            def experts_add(base, e):
                dve.wait_ge(o_ps, base + e + 1)
                for t in range(NT):
                    ins = dve.scalar_tensor_tensor(X[:, t, :], PS[:, 4 + t // 4, 128 * (t % 4):128 * (t % 4) + 128],
                                                   cf[:, t, e:e + 1], X[:, t, :], ALU.mult, ALU.add)
                ins.then_inc(o_add, 1)
                dve.wait_ge(o_add, base + e + 1)

            layernorm(2)
            dve.wait_ge(lg_ps, 2)
            softmax(2)
            first_of(cf, ta, NE, s8[2])
            link(dve.tensor_tensor(cf, cf, s8[2][:, :, None].to_broadcast([128, NT, NE]), ALU.mult))
            dve.tensor_scalar(cf, cf, tg[:, 2:3], None, ALU.mult).then_inc(r_max, 1)
            dve.wait_ge(r_max, 1)
            for e in range(NE):
                experts_add(0, e)

            dve.wait_ge(in_mask, 32)
            link(dve.tensor_copy(capA[0:112], msk8[0:112]))
            link(dve.tensor_scalar(capB[0:112], capA[0:112], 0.5, None, ALU.is_lt))
            link(dve.tensor_reduce(sm[0:56, 576:588], capB[0:56].rearrange("p (c k) -> p c k", c=NC), AX, ALU.max))
            link(dve.tensor_reduce(sm[0:56, 588:589], sm[0:56, 576:588], AX, ALU.max))
            link(dve.tensor_scalar(sm[0:56, 588:589], sm[0:56, 588:589], 0.5, None, ALU.is_lt))
            link(dve.tensor_scalar(capA[0:112], capA[0:112], -1e9, None, ALU.mult))
            dve.scalar_tensor_tensor(cap[0:112], capB[0:112], MAXV, capA[0:112], ALU.mult, ALU.add).then_inc(cap_ok, 1)
            dve.wait_ge(c0_t, 1)
            dve.tensor_reduce(sm[0:13, 592:593], PS[0:13, 0, 0:56], AX, ALU.max).then_inc(c0_f, 1)
            dve.wait_ge(c0_t, 2)
            link(dve.tensor_tensor(sm[0:1, 596:609], PS[0:1, 0, 64:77], C("late")[0:1, 0:13], ALU.mult))
            link(dve.tensor_reduce(sm[0:1, 612:613], sm[0:1, 596:609], AX, ALU.max))
            dve.tensor_copy(live_i[0:1, 0:1], sm[0:1, 612:613]).then_inc(c0_ok, 1)
            dve.wait_ge(c0_ok, 1)
            layernorm(3)
            dve.memset(acc, 0.0)
            link(dve.memset(mrun[:], -MAXV))
            dve.wait_ge(q_ps, 1)
            for i in range(2):
                q = PS[:, i, :].rearrange("p (b q) -> p b q", b=8)[:, :, 0:NQ]
                for h in range(4):
                    last = dve.tensor_scalar(qbd[:, 8 * i:8 * i + 8, h, :], q, S("bq"), C("sel")[:, h:h + 1],
                                             ALU.add, ALU.mult)
            last.then_inc(q_sb, 1)
            live = dve.value_load(live_i[0:1, 0:1], min_val=1, max_val=NC)

            def capped(key, m, u):
                dve.wait_ge(a_s, NT * m + u + 1)
                k = cap[0:112, bass.ds(key, KC)]
                dve.tensor_tensor(sS[0:112].rearrange("p (g r) k -> p g r k", g=4),
                                  PS[0:112, 0:4, 0:CH].rearrange("p g (r k) -> p g r k", k=KC),
                                  k[:, None, None, :].to_broadcast([112, 4, 4, KC]), ALU.min).then_inc(a_min, 1)
                dve.wait_ge(a_min, NT * m + u + 1 + START)

            with dve.Fori(0, live) as n:
                key = dve.snap(n * -KC + (NC - 1) * KC)
                for u in range(NT):
                    dve.wait_ge(a_max, NT * n + u + START)
                    capped(key, n, u)
                    dve.tensor_reduce(mtmp[0:112, u, :], sS[0:112], AX, ALU.max).then_inc(a_max, 1)
                dve.wait_ge(a_max, NT * n + NT + START)
                dve.tensor_tensor(mrun[0:112], mrun[0:112], mtmp[0:112], ALU.max).then_inc(a_end, 1)
                dve.wait_ge(a_end, n + 1)
            with dve.Fori(0, live) as n:
                key = dve.snap(n * -KC + (NC - 1) * KC)
                m = n + live
                for u in range(NT):
                    dve.wait_ge(a_tp, 16 * n + 2 * u + START)
                    capped(key, m, u)
                    dve.tensor_tensor(sS[0:112], sS[0:112],
                                      mrun[0:112, u, :, None].to_broadcast([112, 16, KC]), ALU.subtract).then_inc(a_sub, 1)
                    for h in range(2):
                        b = 2 * u + h
                        dve.wait_ge(a_o, 16 * n + b + 1 + START)
                        dve.tensor_tensor(acc[:, b, :], acc[:, b, :], PS[:, 6, 0:2 * ST], ALU.add).then_inc(a_acc, 1)
            dve.wait_ge(a_acc, live * 16 + START)
            for dst, at in ((oT, 0), (lT, ST)):
                link(dve.memset(dst, 1.0 if at else 0.0))
                d = dst[:, :, 0:NQ]
                for h in range(4):
                    a = acc[:, :, at + NQ * h:at + NQ * h + NQ]
                    if h == 0:
                        link(dve.tensor_scalar(d, a, C("one4")[:, 0:1], None, ALU.mult))
                    else:
                        link(dve.scalar_tensor_tensor(d, a, C("one4")[:, h:h + 1], d, ALU.mult, ALU.add))
            link(dve.reciprocal(lT, lT))
            link(dve.tensor_tensor(oT, oT, lT, ALU.mult))
            dve.tensor_scalar(oT, oT, S("bv"), None, ALU.add).then_inc(a_fin, 1)
            dve.wait_ge(wo_ps, 1)
            Xa = X[:].rearrange("p t d -> p (t d)").rearrange("p (a w) -> p a w", a=2)
            dve.scalar_tensor_tensor(Xa, PS[:, 0:2, :], tg[:, 1:2], Xa, ALU.mult, ALU.add).then_inc(x_up, 1)
            dve.wait_ge(x_up, 2)

            layernorm(4)
            dve.wait_ge(lg_ps, 3)
            softmax(4)
            grp, oh = tb[:, :, 0:4], tc[:, :, 0:4]
            pair = ta.rearrange("p t (g i) -> p t g i", i=2)
            link(dve.tensor_tensor(grp, pair[:, :, :, 0], pair[:, :, :, 1], ALU.max))
            first_of(oh, grp, 4, s8[2])
            link(dve.scalar_tensor_tensor(grp, oh, -2.0, grp, ALU.mult, ALU.add))
            o2 = tb[:, :, 4:8]
            first_of(o2, grp, 4, s8[2])
            link(dve.tensor_tensor(oh, oh, o2, ALU.add))
            link(dve.tensor_tensor(pair, pair, oh[:, :, :, None].to_broadcast([128, NT, 4, 2]), ALU.mult))
            first_of(tb, ta, NE, s8[2])
            link(dve.scalar_tensor_tensor(cf, tb, -2.0, ta, ALU.mult, ALU.add))
            first_of(tc, cf, NE, s8[3])
            link(dve.tensor_tensor(s8[2], s8[2], s8[3], ALU.add))
            link(dve.reciprocal(s8[3], s8[2]))
            link(dve.tensor_tensor(tb, tb, tc, ALU.add))
            link(dve.tensor_tensor(cf, tb, ta, ALU.mult))
            link(dve.tensor_tensor(cf, cf, s8[3][:, :, None].to_broadcast([128, NT, NE]), ALU.mult))
            dve.tensor_scalar(cf, cf, tg[:, 3:4], None, ALU.mult).then_inc(r_max, 1)
            dve.wait_ge(r_max, 2)
            for e in range(NE):
                for a in range(2):
                    n = 2 * e + a
                    dve.wait_ge(h_act, 2 * NE + n + 1)
                    if e >= 2:
                        dve.wait_ge(o_ps, NE + e - 1)
                    dve.tensor_tensor(gT[:, e % 2, a, :].rearrange("p (i t) -> p i t", i=2),
                                      sil[:, a, :].rearrange("p (i t) -> p i t", i=2), PS[:, 2:4, :], ALU.mult).then_inc(h_mul, 1)
                experts_add(NE, e)


def kernel(**inputs):
    import concourse.bacc as _bacc
    from concourse.bass_utils import run_bass_kernel_spmd as _run

    a = {k: np.asarray(v) for k, v in inputs.items()}
    ctx = np.ascontiguousarray(a["ctx_1024"])
    parts = {"wq": a["L1_xattn_W_q"], "wk": a["L1_xattn_W_k"], "wv": a["L1_xattn_W_v"], "wo": a["L1_xattn_W_o"],
             "wred": a["L0_ffn_w_red"], "gate": a["L1_ffn_gate_w"].T, "bq": a["L1_xattn_b_q"][:, None],
             "bk": a["L1_xattn_b_k"][:, None], "bv": a["L1_xattn_b_v"][:, None],
             "b1": a["L0_ffn_b1"].reshape(2 * NE, 128).T,
             "g": np.broadcast_to(np.concatenate([a["g_xattn"], a["g_ffn"]])[None, :], (128, 4))}
    arrays = {
        "x": a["x"],
        "ctx": ctx,
        "ctxT": ctx.transpose(0, 2, 1),
        "mask": a["mask_1x1xSxS2_bk1"].reshape(NQ, NK),
        "cst": const_values(),
        "small": np.concatenate([parts[n] for n, _ in SMALL], axis=1),
        "rows": np.concatenate([a["L0_ffn_b2"].reshape(1, -1), a["L1_xattn_b_o"][None, :]], axis=1),
        "wg": a["L0_ffn_wg"],
        "w1": a["L0_ffn_W1"],
        "w2": a["L0_ffn_W2"].reshape(2 * NE, 128, 128).transpose(1, 0, 2),
        "w13": a["L1_ffn_w13_weight"].transpose(2, 0, 1),
        "w2b": a["L1_ffn_w2_weight"].transpose(0, 2, 1).reshape(2 * NE, 128, 128).transpose(1, 0, 2),
    }
    nc = _bacc.Bacc("TRN2", target_bir_lowering=False, num_devices=1)
    fed, args = {}, []
    for name, v in arrays.items():
        v = np.ascontiguousarray(v)
        fed[f"in_{name}"] = v
        args.append(nc.dram_tensor(f"in_{name}", v.shape, mybir.dt.from_np(v.dtype), kind="ExternalInput").ap())
    out = nc.dram_tensor("out_0", (NB, NQ, ND), F32, kind="ExternalOutput").ap()
    flamingo(nc, *args, out)
    r = _run(nc, [fed], core_ids=[0])
    return r.results[0]["out_0"]
```

```python
from contextlib import ExitStack

import numpy as np
import concourse.bass as bass
from concourse import mybir

ALU = mybir.AluOpType
ACT = mybir.ActivationFunctionType
F32 = mybir.dt.float32
I32 = mybir.dt.int32
U8 = mybir.dt.uint8
AX = mybir.AxisListType.X

NB, NQ, ND, NK = 16, 56, 128, 1500
NT = NB // 2
NE = 8
NH, DH = 16, 8
BIG = 1e30
NBLK = 8
BR = -(-NK // NBLK)
LAG = 2
SLOTS = 1 + NQ + LAG * (NBLK - 1)
SW = BR + 1
VG = 7
RING = 4
DIAG = 2.0 ** -12
TINY = 1e-30
KC, NC = 125, 12
CH = 500
MAXV = 3e38
EPS = 1e-5
START = 8
ST = NH * NQ // 4


def const_layout():
    names = [("ident", 128), ("shift", 128), ("same", 128), ("ones", 128), ("rows", BR), ("edge", 1),
             ("first", SW), ("sel", 4), ("key", NC), ("rank8", 8), ("rank4", 8), ("late", 16), ("blk", NBLK), ("half", 2), ("zero", 128), ("tiny", 1), ("keyh", NC)]
    at, out = 0, {}
    for n, w in names:
        out[n] = (at, w)
        at += w
    return out, at


def const_values():
    lay, width = const_layout()
    c = np.zeros((128, width), np.float32)
    p = np.arange(128)

    def put(name, v):
        a, w = lay[name]
        c[:, a:a + w] = v

    put("ident", np.eye(128))
    put("shift", (p[None, :] == p[:, None] + 16))
    put("same", (p[None, :] % 16 == p[:, None] % 16))
    put("ones", 1.0)
    put("rows", BR * (p[:, None] // 16) + np.arange(BR)[None, :])
    put("edge", np.where(p[:, None] < 16, BIG, 0.0))
    first = np.full((128, SW), BIG)
    first[:16, 0] = 0.0
    put("first", first)
    inh = (p[:, None] % 32) // DH == np.arange(4)[None, :]
    put("sel", inh / np.sqrt(np.float32(DH)))
    put("half", np.stack([p < NQ, p >= NQ], 1))
    put("key", NC * p[:, None] + np.arange(NC)[None, :])
    put("keyh", NC * p[:, None] + np.arange(NC)[None, :] + 0.5)
    put("tiny", TINY)
    put("rank8", NE - np.arange(8))
    put("rank4", np.r_[4 - np.arange(4), np.zeros(4)])
    put("blk", p[:, None] // 16 == np.arange(NBLK)[None, :])
    put("late", np.r_[NC - np.arange(NC), NC, np.zeros(3)])
    return c


SMALL = [("wq", 128), ("wk", 128), ("wv", 128), ("wred", 16), ("gate", 8), ("bq", 1), ("bk", 1),
         ("b1", 16), ("g", 4)]
VW = 2 * DH + 1


def small_layout():
    at, out = 0, {}
    for n, w in SMALL:
        out[n] = (at, w)
        at += w
    return out, at


def flamingo(nc, x, ctx, ctxT, mask, cst_h, small_h, bo_h, wg, pair_h, b2_h, w1, w2, w13, w2b, out):
    st = ExitStack()
    clay, cw = const_layout()
    slay, sw = small_layout()
    with st:
        def sb(name, shape, dt=F32):
            return st.enter_context(nc.sbuf_tensor(name, shape, dt))

        def sem(name):
            return st.enter_context(nc.semaphore(name))

        cst = sb("cst", [128, cw])
        small = sb("small", [128, sw])
        bo = sb("bo", [1, 128])
        pair = sb("pair", [64, 258])
        wg_s = sb("wg_s", [NE, 16])
        W1 = sb("W1", [128, NE, 256])
        W2 = sb("W2", [128, 2 * NE, 128])
        X = sb("X", [128, NT, 128])
        H = sb("H", [128, NT, 128])
        SQ = sb("SQ", [128, NT, 128])
        HT = sb("HT", [128, NT, 128])
        st8 = sb("st8", [128, 6, NT])
        R = sb("R", [128, SLOTS * SW])
        VM = sb("VM", [128, NC * NB * 56])
        CA = sb("CA", [128, 8 * NC * 128])
        best = sb("best", [128, RING, BR])
        diag = sb("diag", [128, RING, BR])
        over = sb("over", [128, RING, BR])
        mrow = sb("mrow", [128, BR])
        sm = sb("sm", [128, 640])
        live_i = sb("live_i", [1, 4], I32)
        PS = st.enter_context(nc.psum_tensor("PS", [128, 8, 512], F32))

        def C(n):
            a, w = clay[n]
            return cst[:, a:a + w]

        def S(n):
            a, w = slay[n]
            return small[:, a:a + w]

        def small_area(a, w):
            return sm[:, a:a + w]

        Rv = R[:].rearrange("p (t c) -> p t c", c=SW)
        Vcol = VM[:, 0:NQ * BR].rearrange("p (j r) -> p j r", r=BR)
        Mk = VM[:].rearrange("p (c b q) -> p c b q", c=NC, b=NB)
        cT = CA[:, 0:6000].rearrange("p (n k) -> p n k", n=4)
        cSq = CA[:, 6000:9000].rearrange("p (n k) -> p n k", n=2)
        Dt = CA[:, 9000:12000].rearrange("p (n k) -> p n k", n=2)
        nat = [CA[:, 0:8 * NC * 128].rearrange("p (b c d) -> p b c d", b=8, c=NC),
               R[:, 0:8 * NC * 128].rearrange("p (b c d) -> p b c d", b=8, c=NC)]
        gT = CA[:, 0:3072].rearrange("p (n a t) -> p n a t", n=3, a=2)
        sil = CA[:, 3072:4096].rearrange("p (n t) -> p n t", n=2)
        b2d = CA[0:64, 4096:5120]
        cfT = CA[0:64, 5120:5248]
        acc = R[:, 0:NT * 16 * VW].rearrange("p (u g v) -> p u g v", u=NT, g=16)
        pT = R[:, 2176:2176 + 2 * 1792].rearrange("p (n k) -> p n k", n=2)
        qbd = R[:, 7168:7168 + NB * 4 * NQ].rearrange("p (b h q) -> p b h q", b=NB, h=4)
        oN = R[:, 5760:5760 + 1024].rearrange("p (h g d) -> p h g d", h=2, d=DH)
        cap = R[:, 10752:12252]
        ckT = CA[:, 5248:7248].rearrange("p (b k) -> p b k", b=NB)
        kT = CA[:, 7248:9248].rearrange("p (b k) -> p b k", b=NB)
        sS = CA[:, 0:4000].rearrange("p (n g k) -> p n g k", n=2, g=16)
        W13 = VM[:, 0:4096].rearrange("p (e i) -> p e i", e=NE)
        W2B = VM[:, 4096:6144].rearrange("p (e i) -> p e i", e=2 * NE)
        oT = VM[0:64, 6144:6144 + 2048].rearrange("p (h b q) -> p h b q", h=2, b=NB)
        vC = VM[:, 8192:8192 + NB * 8 * VW].rearrange("p (b g v) -> p b g v", b=NB, g=8)
        msk8 = CA[:, 9248:9623].bitcast(U8)
        capA = CA[:, 9623:11123]
        capB = VM[:, 9000:10500]

        tg = small_area(0, 4)
        E = small_area(8, NQ + 1)
        vmax = small_area(72, 1)
        e8 = small_area(76, NBLK)
        wgn = small_area(96, 16)
        wgs = small_area(112, 4)
        wgT = small_area(116, 8)
        lg = small_area(128, 64).rearrange("p (t e) -> p t e", t=NT)
        cf = small_area(192, 64).rearrange("p (t e) -> p t e", t=NT)
        ta = small_area(256, 64).rearrange("p (t e) -> p t e", t=NT)
        tb = small_area(320, 64).rearrange("p (t e) -> p t e", t=NT)
        tc = small_area(384, 64).rearrange("p (t e) -> p t e", t=NT)
        td = small_area(448, 64).rearrange("p (t e) -> p t e", t=NT)
        mrun = sb("mrun", [128, NT, 16])
        mtmp = sb("mtmp", [128, 2, 16])
        mnew = sb("mnew", [128, 2, 16])
        drop = sb("drop", [128, 2, 16])
        alpha = sb("alpha", [128, 2, 16])
        bnst = sb("bnst", [128, NT, 6])
        mv = sb("mv", [128, NT, 2])
        Eb = sb("Eb", [128, NB * (NQ + 1)])
        Ed = SQ[:].rearrange("p t d -> p (t d)")[:, 0:NB * (NQ + 1)]
        G1 = H[:].rearrange("p t d -> p (t d)")[:, 0:NB * NQ]
        Ebv = Eb[:].rearrange("p (b j) -> p b j", b=NB)

        in_cst = sem("in_cst")
        in_x = sem("in_x")
        in_w = sem("in_w")
        in_ct = [sem(f"in_ct{i}") for i in range(4)]
        in_nat = sem("in_nat")
        in_nat2 = sem("in_nat2")
        in_w13 = sem("in_w13")
        in_mask = sem("in_mask")
        vec = sem("vec_step")
        pool_init = sem("pool_init")
        ln_var = sem("ln_var")
        ln_std = sem("ln_std")
        ln_out = sem("ln_out")
        ht_ps = sem("ht_ps")
        ht_sb = sem("ht_sb")
        sq_ok = sem("ctx_squared")
        d_ps = sem("dist_psum")
        d_add = sem("dist_added")
        d_root = sem("dist_root")
        d_put = [[sem(f"dist_placed{i}_{h}") for h in range(2)] for i in range(2)]
        w_min = sem("wave_min")
        w_row = sem("wave_row")
        w_shift = sem("wave_shifted")
        w_edge = sem("wave_edge")
        v_y = sem("choice_left_over")
        v_z = sem("choice_diagonal")
        v_x = sem("choice_difference")
        v_f = sem("choice_factor")
        v_q = sem("choice_tie")
        v_u = sem("choice_made")
        v_put = sem("choice_placed")
        b_g = sem("back_mask")
        b_max = sem("back_blockmax")
        b_t = sem("back_transposed")
        b_e = sem("back_max")
        b_bc = sem("back_threshold")
        e_tab = sem("e_diag")
        e_bc = sem("e_broadcast")
        m_ok = sem("path_mask")
        x_ps = sem("aligned_psum")
        x_up = sem("x_updated")
        wg_t = sem("router_transposed")
        wg_r = sem("router_ready")
        wg_sq = sem("router_squares")
        wg_std = sem("router_norms")
        lg_ps = sem("logits_psum")
        lg_rd = sem("router_reduced")
        r_max = sem("route_max")
        r_exp = sem("route_exp")
        h_ps = sem("hidden_psum")
        h_act = sem("hidden_act")
        h_mul = sem("hidden_mul")
        o_ps = sem("expert_psum")
        o_add = sem("expert_added")
        tanh_ok = sem("gates_tanh")
        q_ps = sem("query_psum")
        q_sb = sem("query_blocks")
        cap_ok = sem("mask_cap")
        live_t = sem("live_psum")
        live_f = sem("live_flags")
        live_ok = sem("live_chunks")
        a_in = sem("attn_ctx_in")
        a_kps = sem("attn_k_psum")
        a_kT = sem("attn_k")
        a_vps = sem("attn_v_psum")
        a_v = sem("attn_v")
        a_s = sem("attn_scores")
        a_min = sem("attn_capped")
        a_max = sem("attn_max")
        a_mr = sem("attn_running_max")
        a_sub = sem("attn_shifted")
        a_al = sem("attn_rescale")
        a_am = sem("attn_rescaled")
        a_tps = sem("attn_out_transposed")
        a_oT = sem("attn_out_T")
        pool_late = sem("pool_late")
        pool_one = sem("pool_ones")
        b2_ok = sem("bias_psum")
        b2_t = sem("bias_coeff_T")
        in_b2 = sem("in_b2")
        a_exp = sem("attn_exp")
        a_tp = sem("attn_p_transposed")
        a_pT = sem("attn_pT")
        a_o = sem("attn_out_psum")
        a_acc = sem("attn_accumulated")
        a_fin = sem("attn_norm")
        wo_ps = sem("attn_projected")
        out_s = sem("out_stored")

        block = st.enter_context(nc.Block())
        NLN = 4

        def columns_of(t0, t1):
            for k in range(NBLK):
                a = max(t0, 2 + LAG * k)
                b = min(t1, NQ + 1 + LAG * k)
                if a < b:
                    yield k, a - 1, b - a, a - 1 - LAG * k
        groups = [(a, min(a + VG, SLOTS)) for a in range(1, SLOTS, VG)]
        puts = sum(sum(1 for _ in columns_of(*g)) for g in groups)

        @block.sync
        def _(sp):
            sp.dma_start(cst[:], cst_h).then_inc(in_cst, 16)
            xs = x.rearrange("(t h) q d -> h q t d", h=2)
            sp.wait_ge(pool_init, 1)
            sp.dma_start(X[0:NQ, :, :], xs[0]).then_inc(in_x, 16)
            sp.dma_start(X[64:64 + NQ, :, :], xs[1]).then_inc(in_x, 16)
            sp.dma_start(small[:], small_h).then_inc(in_cst, 16)
            for b in range(4):
                sp.dma_start(cT[:, b, :], ctxT[b]).then_inc(in_ct[b], 16)
            sp.dma_start(bo[:], bo_h).then_inc(in_w, 16)
            sp.dma_start(wg_s[:], wg).then_inc(in_w, 16)
            sp.dma_start(W1[:], w1.rearrange("e c h -> c e h")).then_inc(in_w, 16)
            sp.dma_start(W2[:], w2).then_inc(in_w, 16)
            sp.dma_start(pair[:], pair_h).then_inc(in_w, 16)
            for u in range(NT):
                sp.wait_ge(d_root, u + 1)
                if u == 0:
                    sp.wait_ge(pool_init, 2)
                for k in range(NBLK):
                    n = min(BR, NK - BR * k)
                    p = 16 * k + 2 * u
                    sp.dma_start(Rv[p:p + 1, 1 + LAG * k:1 + LAG * k + NQ, 1:1 + n],
                                 Dt[0:NQ, u % 2, BR * k:BR * k + n]).then_inc(d_put[u % 2][0], 16)
                for b in (2 * u + 4, 2 * u + 5):
                    if b < NB:
                        sp.wait_ge(d_ps, u + 1)
                        sp.dma_start(cT[:, b % 4, :], ctxT[b]).then_inc(in_ct[b % 4], 16)
            for i in range(2):
                for h in range(2):
                    sp.wait_ge(d_put[i][h], 16 * NBLK * NT // 2)
            sp.dma_start(nat[0][0:KC], ctx.rearrange("b (p c) d -> p b c d", c=NC)[:, 0:8]).then_inc(in_nat, 16)
            for t0, t1 in groups:
                sp.wait_ge(v_u, t1 - 1)
                for k, a, n, j in columns_of(t0, t1):
                    sp.dma_start(Vcol[16 * k:16 * k + 16, j:j + n, :],
                                 Rv[16 * k:16 * k + 16, a:a + n, 1:SW]).then_inc(v_put, 16)
            sp.wait_ge(v_put, 16 * puts)
            sp.dma_start(nat[1][0:KC], ctx.rearrange("b (p c) d -> p b c d", c=NC)[:, 8:16]).then_inc(in_nat2, 16)
            sp.wait_ge(x_ps, 1)
            sp.dma_start(W13, w13).then_inc(in_w13, 16)
            sp.dma_start(W2B, w2b).then_inc(in_w13, 16)
            sp.dma_start(b2d, b2_h).then_inc(in_b2, 16)
            for h in range(2):
                sp.dma_start(msk8[NQ * h:NQ * h + NQ, :], mask).then_inc(in_mask, 16)
            sp.wait_ge(live_ok, 1)
            live = sp.value_load(live_i[0:1, 0:1], min_val=1, max_val=NC)
            with sp.Fori(0, live) as n:
                key = sp.snap(n * -KC + (NC - 1) * KC)
                sp.wait_ge(a_vps, 4 * n + START)
                sp.dma_start(ckT, ctxT.rearrange("b d k -> d b k")[:, :, bass.ds(key, KC)]).then_inc(a_in, 16)
            sp.wait_ge(o_add, 4 * NE)
            os = out.rearrange("(t h) q d -> h q t d", h=2)
            sp.dma_start(os[0], X[0:NQ, :, :]).then_inc(out_s, 16)
            sp.dma_start(os[1], X[64:64 + NQ, :, :]).then_inc(out_s, 16)
            sp.wait_ge(out_s, 32)

        @block.gpsimd
        def _(pool):
            for s in (a_min, a_max, a_tp, a_acc, a_o, a_pT, a_vps, a_mr, a_am):
                pool.sem_inc(s, START)
            pool.memset(X[:], 0.0).then_inc(pool_init, 1)
            pool.memset(R[:], BIG).then_inc(pool_init, 1)
            pool.wait_ge(pool_init, 2)
            for u in range(NT):
                pool.wait_ge(d_root, u + 1)
                for k in range(NBLK):
                    n = min(BR, NK - BR * k)
                    p = 16 * k + 2 * u + 1
                    pool.dma_start(Rv[p:p + 1, 1 + LAG * k:1 + LAG * k + NQ, 1:1 + n],
                                   Dt[64:64 + NQ, u % 2, BR * k:BR * k + n]).then_inc(d_put[u % 2][1], 16)
            for t in range(1, SLOTS):
                pool.wait_ge(w_row, t)
                if t > RING:
                    pool.wait_ge(v_u, t - RING)
                pool.tensor_tensor(diag[:, t % RING, :], Rv[:, t - 1, 1:SW], Rv[:, t - 1, 0:BR], ALU.subtract).then_inc(v_y, 1)
                pool.wait_ge(w_row, t + 1)
                pool.tensor_tensor(over[:, t % RING, :], Rv[:, t, 0:BR], best[:, t % RING, :], ALU.subtract).then_inc(v_x, 1)
            pool.wait_ge(x_ps, 1)
            pool.memset(gT.rearrange("p n a (b q) -> p (n a b) q", q=64)[:, :, NQ:64], 0.0)
            pool.memset(acc, 0.0)
            pool.memset(oT, 0.0)
            pool.memset(mrun[:], -MAXV).then_inc(pool_late, 1)
            pool.wait_ge(cap_ok, 1)
            pool.memset(vC, 1.0).then_inc(pool_one, 1)
            pool.wait_ge(live_ok, 1)
            live = pool.value_load(live_i[0:1, 0:1], min_val=1, max_val=NC)
            with pool.Fori(0, live) as n:
                for u in range(NT):
                    pool.wait_ge(a_max, 3 * NT * n + 3 * u + 2 + START)
                    pool.tensor_tensor(sS[0:112, u % 2], sS[0:112, u % 2],
                                       mnew[0:112, u % 2, :, None].to_broadcast([112, 16, KC]),
                                       ALU.subtract).then_inc(a_sub, 1)
                    pool.wait_ge(a_max, 3 * NT * n + 3 * u + 3 + START)
                    pool.tensor_tensor(mrun[0:112, u, :], mnew[0:112, u % 2, :], C("ones")[0:112, 0:16], ALU.mult).then_inc(a_mr, 1)

        @block.tensor
        def _(pe):
            ident = C("ident")

            def transposes(n):
                pe.wait_ge(ln_out, n + 1)
                if n == 1:
                    pe.wait_ge(x_up, 1)
                for t in range(NT):
                    last = pe.transpose(PS[:, 6 + t // 4, 128 * (t % 4):128 * (t % 4) + 128], H[:, t, :], ident)
                last.then_inc(ht_ps, 1)

            pe.wait_ge(in_cst, 32)
            transposes(0)
            pe.wait_ge(ht_sb, 2)
            for u in range(NT):
                if u >= 2:
                    pe.wait_ge(d_add, u - 1)
                if u == 1:
                    pe.wait_ge(d_add, 1)
                for h in range(2):
                    b = 2 * u + h
                    pe.wait_ge(sq_ok, b + 1)
                    pe.wait_ge(in_ct[b % 4], 16 * (b // 4 + 1))
                    for i in range(3):
                        o = PS[64 * h:64 * h + 64, 3 * (u % 2) + i, 0:CH]
                        pe.matmul(o, C("ones")[:, 0:64], cSq[:, h, CH * i:CH * i + CH], start=True, stop=False)
                        last = pe.matmul(o, HT[:, u, 64 * h:64 * h + 64], cT[:, b % 4, CH * i:CH * i + CH],
                                         start=False, stop=True)
                last.then_inc(d_ps, 1)
            pe.wait_ge(d_add, NT)
            for t in range(SLOTS - 2):
                pe.wait_ge(w_row, t + 1)
                if t:
                    pe.wait_ge(w_edge, t)
                pe.matmul(PS[:, 0, t:t + 1], C("shift"), Rv[:, t, BR:BR + 1], start=True, stop=True).then_inc(w_shift, 1)
            for n in range(NQ - 1):
                pe.wait_ge(b_t, n + 1)
                pe.matmul(PS[:, 1, bass.ds(n * NBLK, NBLK)], C("same"), e8, start=True, stop=True).then_inc(b_bc, 1)
            pe.wait_ge(e_tab, 1)
            W = NB * (NQ + 1) // 2
            for i in range(2):
                last = pe.matmul(PS[:, 3 + i, 0:W], C("ones")[0:16, :], Ed[0:16, W * i:W * i + W],
                                 start=True, stop=True)
            last.then_inc(e_bc, 1)
            for i in range(2):
                pe.matmul(PS[:, 5 + i, :], C("zero")[0:1, :], X[0:1, 0:4, :], start=True, stop=False,
                          skip_group_check=True)
            pe.wait_ge(in_nat, 16)
            pe.wait_ge(in_nat2, 16)
            for c in range(NC):
                pe.wait_ge(m_ok, c + 1)
                for b in range(NB):
                    t, h = b // 2, b % 2
                    last = pe.matmul(PS[64 * h:64 * h + NQ, 5 + t // 4, 128 * (t % 4):128 * (t % 4) + 128],
                                     Mk[0:KC, c, b, :], nat[b // 8][0:KC, b % 8, c, :],
                                     start=False, stop=(c == NC - 1), skip_group_check=True)
            last.then_inc(x_ps, 1)

            def tokens(th):
                return HT[:, 4 * th:4 * th + 4, :].rearrange("p t (h q) -> p (t h) q", h=2)[:, :, 0:NQ]

            def out_group(i, w, ready):
                pe.wait_ge(ready, 2 * i + 2)
                e, th = i // 2, i % 2
                for t in range(4):
                    for a in range(2):
                        last = pe.matmul(PS[:, 6 + th, 128 * t:128 * t + 128], gT[:, i % 3, a, 128 * t:128 * t + 128],
                                         w[:, 2 * e + a, :], start=(a == 0), stop=(a == 1))
                last.then_inc(o_ps, 1)

            pe.wait_ge(in_w, 80)
            pe.wait_ge(wg_r, 1)
            pe.transpose(PS[0:16, 3, 0:8], wgn[0:8, :], C("ident")[0:8, 0:8]).then_inc(wg_t, 1)
            transposes(1)
            pe.wait_ge(ht_sb, 3)
            for t in range(2):
                last = pe.matmul(PS[0:16, t, :], S("wred"), HT[:, 4 * t:4 * t + 4, :], start=True, stop=True)
            last.then_inc(lg_ps, 1)
            pe.wait_ge(lg_rd, 2)
            for t in range(NT):
                last = pe.matmul(PS[:, 5, 64 + 8 * t:72 + 8 * t], SQ[0:16, t, :], wgT[0:16, :], start=True, stop=True)
            last.then_inc(lg_ps, 1)
            def hidden_a(i):
                e, th = i // 2, i % 2
                for a in range(2):
                    m = 2 * i + a
                    if m >= 4:
                        pe.wait_ge(h_act, m - 3)
                    pe.matmul(PS[:, m % 4, 0:448], W1[:, e, 128 * a:128 * a + 128], tokens(th),
                              start=True, stop=True).then_inc(h_ps, 1)

            hidden_a(0)
            for i in range(2 * NE):
                if i + 1 < 2 * NE:
                    hidden_a(i + 1)
                if i >= 2:
                    pe.wait_ge(o_add, i - 1)
                out_group(i, W2, h_act)
                if i == 3:
                    pe.wait_ge(r_max, 1)
                    pe.transpose(PS[0:64, 4, 0:128], cf.rearrange("p t e -> p (t e)"), ident).then_inc(b2_ok, 1)
                if i == 5:
                    pe.wait_ge(b2_t, 1)
                    pe.wait_ge(in_b2, 16)
                    for t in range(2):
                        last = pe.matmul(PS[:, 4 + t, :], cfT, b2d[:, 512 * t:512 * t + 512], start=True, stop=True)
                    last.then_inc(b2_ok, 1)

            pe.wait_ge(cap_ok, 1)
            pe.transpose(PS[0:13, 0, 0:56], sm[0:56, 576:589], C("ident")[0:56, 0:56]).then_inc(live_t, 1)
            pe.wait_ge(live_f, 1)
            pe.transpose(PS[0:1, 0, 64:77], sm[0:13, 592:593], C("ident")[0:13, 0:13]).then_inc(live_t, 1)
            pe.wait_ge(live_ok, 1)
            transposes(2)
            pe.wait_ge(ht_sb, 4)
            for t in range(2):
                last = pe.matmul(PS[:, t, :], S("wq"), HT[:, 4 * t:4 * t + 4, :], start=True, stop=True)
            last.then_inc(q_ps, 1)
            pe.wait_ge(q_sb, 1)
            pe.wait_ge(live_ok, 1)
            live = pe.value_load(live_i[0:1, 0:1], min_val=1, max_val=NC)

            def scores(N, n, u):
                pe.wait_ge(a_v, 4 * n + 4)
                pe.wait_ge(a_min, N + START)
                for h in range(2):
                    for g in range(4):
                        for pr in range(2):
                            k = 2 * pr + h
                            last = pe.matmul(PS[0:112, g, KC * k:KC * k + KC],
                                             qbd[32 * g:32 * g + 32, 2 * u + h, 2 * pr:2 * pr + 2, :],
                                             kT[32 * g:32 * g + 32, 2 * u + h, :], start=True, stop=True,
                                             tile_position=(32 * g, 0))
                last.then_inc(a_s, 1)

            with pe.Fori(0, live) as n:
                pe.wait_ge(a_in, 16 * n + 16)
                pe.wait_ge(a_min, NT * n + START)
                for i in range(4):
                    last = pe.matmul(PS[:, i, 0:CH], S("wk"), ckT[:, 4 * i:4 * i + 4, :], start=True, stop=True)
                last.then_inc(a_kps, 1)
                for i in range(4):
                    pe.wait_ge(a_kT, 4 * n + i + 1)
                    for b in range(4):
                        last = pe.matmul(PS[0:KC, i, 128 * b:128 * b + 128], ckT[:, 4 * i + b, :], S("wv"),
                                         start=True, stop=True)
                    last.then_inc(a_vps, 1)
                scores(NT * n, n, 0)
                for u in range(NT):
                    N = NT * n + u
                    if u + 1 < NT:
                        scores(N + 1, n, u + 1)
                    pe.wait_ge(a_exp, N + 1)
                    for g in range(4):
                        pe.wait_ge(a_pT, 4 * N + (g - 2 if u else max(g - 2, 0)) + START)
                        for k in range(4):
                            last = pe.transpose(PS[0:KC, 4 + (4 * u + g) % 3, 112 * k:112 * k + 112],
                                                sS[0:112, u % 2, 4 * g + k, :], C("ident")[0:112, 0:112])
                        last.then_inc(a_tp, 1)
                    pe.wait_ge(a_pT, 4 * N + 4 + START)
                    pe.wait_ge(a_acc, N + START)
                    for g in range(4):
                        for k in range(4):
                            b, pr = 2 * u + k % 2, k // 2
                            j = 4 * g + k
                            last = pe.matmul(PS[0:112, 7, VW * j:VW * j + VW],
                                             pT[0:KC, u % 2, 448 * g + 112 * k:448 * g + 112 * k + 112],
                                             vC[0:KC, b, 2 * g + pr, :], start=True, stop=True)
                    last.then_inc(a_o, 1)
            pe.wait_ge(a_fin, 1)
            for b in range(NB):
                last = pe.transpose(PS[0:64, b // 4, 112 * (b % 4):112 * (b % 4) + 112],
                                    oN[0:112, b % 2, 4 * (b // 2) * 2:4 * (b // 2) * 2 + 8, :].rearrange("p g d -> p (g d)"),
                                    C("ident")[0:112, 0:112])
            last.then_inc(a_tps, 1)
            pe.wait_ge(a_oT, 2)
            for t in range(NT):
                o = PS[:, 4 + t // 4, 128 * (t % 4):128 * (t % 4) + 128]
                for h in range(2):
                    pe.matmul(o, oT[:, h, 2 * t:2 * t + 2, :].rearrange("p b q -> p (b q)"),
                              pair[:, 128 * h:128 * h + 128], start=(h == 0), stop=False)
                last = pe.matmul(o, C("ones")[0:1, :], bo[:], start=False, stop=True)
            last.then_inc(wo_ps, 1)

            pe.wait_ge(in_w13, 32)
            transposes(3)
            pe.wait_ge(ht_sb, 5)
            for t in range(NT):
                last = pe.matmul(PS[:, 5, 64 + 8 * t:72 + 8 * t], HT[:, t, :], S("gate"), start=True, stop=True)
            last.then_inc(lg_ps, 1)
            def hidden_b(i):
                e, th = i // 2, i % 2
                for a in range(2):
                    m = 2 * i + a
                    if m >= 3:
                        pe.wait_ge(h_mul, m - 2)
                    pe.matmul(PS[:, 2 * (m % 3), 0:448], W13[:, e, 128 * a:128 * a + 128], tokens(th),
                              start=True, stop=True)
                    pe.matmul(PS[:, 2 * (m % 3) + 1, 0:448], W13[:, e, 256 + 128 * a:384 + 128 * a], tokens(th),
                              start=True, stop=True).then_inc(h_ps, 1)

            hidden_b(0)
            pe.wait_ge(r_max, 2)
            for i in range(2 * NE):
                if i + 1 < 2 * NE:
                    hidden_b(i + 1)
                pe.wait_ge(o_add, 2 * NE + max(i - 1, 0))
                out_group(i, W2B, h_mul)

        @block.scalar
        def _(act):
            act.wait_ge(in_cst, 32)
            act.activation(tg, S("g"), ACT.Tanh).then_inc(tanh_ok, 1)

            def root(n):
                act.wait_ge(ln_var, n)
                act.activation(st8[:, 3, :], st8[:, 2, :], ACT.Sqrt).then_inc(ln_std, 1)

            def copy_ht(n, scale):
                act.wait_ge(ht_ps, n)
                act.activation(HT[:], PS[:, 6:8, :].rearrange("p a (t d) -> p (a t) d", d=128), ACT.Copy,
                               scale=scale).then_inc(ht_sb, 2 if n == 1 else 1)

            root(1)
            copy_ht(1, -2.0)
            for b in range(NB):
                u = b // 2
                act.wait_ge(in_ct[b % 4], 16 * (b // 4 + 1))
                if b >= 2:
                    act.wait_ge(d_ps, u)
                act.activation(cSq[:, b % 2, :], cT[:, b % 4, :], ACT.Square).then_inc(sq_ok, 1)
                if b % 2 == 0 and u:
                    act.wait_ge(d_add, u)
                    act.activation(Dt[:, (u - 1) % 2, :], Dt[:, (u - 1) % 2, :], ACT.Sqrt).then_inc(d_root, 1)
            act.wait_ge(d_add, NT)
            act.activation(Dt[:, (NT - 1) % 2, :], Dt[:, (NT - 1) % 2, :], ACT.Sqrt).then_inc(d_root, 1)
            for t in range(1, SLOTS):
                if t < SLOTS - 1:
                    act.wait_ge(w_shift, t)
                    act.activation(Rv[:, t + 1, 0:1], PS[:, 0, t - 1:t],
                                   ACT.Identity, bias=C("edge")).then_inc(w_edge, 1)
                act.wait_ge(w_min, t)
                act.wait_ge(v_y, t)
                act.activation(diag[:, t % RING, :], diag[:, t % RING, :], ACT.Sign, bias=C("tiny")).then_inc(v_z, 1)
                act.wait_ge(v_z, t)
                act.activation(Rv[:, t - 1, 1:SW], diag[:, t % RING, :], ACT.Identity,
                               bias=C("ones")[:, 0:1], scale=-DIAG).then_inc(v_f, 1)
            act.wait_ge(wg_sq, 1)
            act.activation(wgs[0:8, 1:2], wgs[0:8, 0:1], ACT.Sqrt).then_inc(wg_std, 1)
            act.wait_ge(wg_t, 1)
            act.activation(wgT[0:16, :], PS[0:16, 3, 0:8], ACT.Copy).then_inc(lg_rd, 1)
            root(2)
            copy_ht(2, 1.0)
            act.wait_ge(lg_ps, 1)
            act.activation(SQ[0:16, :, :], PS[0:16, 0:2, :].rearrange("p a (t d) -> p (a t) d", d=128),
                           ACT.Copy).then_inc(lg_rd, 1)
            act.wait_ge(r_exp, 1)
            act.activation(ta, lg, ACT.Exp).then_inc(r_exp, 1)
            def units(t):
                return t.rearrange("p (b q) -> p b q", q=64)[:, :, 0:NQ]

            act.wait_ge(pool_late, 1)
            for i in range(2 * NE):
                for a in range(2):
                    m = 2 * i + a
                    act.wait_ge(h_ps, m + 1)
                    if i >= 3:
                        act.wait_ge(o_ps, i - 2)
                    act.activation(units(gT[:, i % 3, a, :]), PS[:, m % 4, 0:448].rearrange("p (b q) -> p b q", q=NQ),
                                   ACT.Gelu, bias=S("b1")[:, 2 * (i // 2) + a:2 * (i // 2) + a + 1]).then_inc(h_act, 1)
                if i == 4:
                    act.wait_ge(b2_ok, 1)
                    act.activation(cfT, PS[0:64, 4, 0:128], ACT.Copy).then_inc(b2_t, 1)
            root(3)
            copy_ht(3, 1.0)
            act.wait_ge(live_ok, 1)
            live = act.value_load(live_i[0:1, 0:1], min_val=1, max_val=NC)
            act.wait_ge(pool_one, 1)
            with act.Fori(0, live) as n:
                for i in range(4):
                    act.wait_ge(a_kps, n + 1)
                    act.activation(kT[:, 4 * i:4 * i + 4, :], PS[:, i, 0:CH].rearrange("p (b k) -> p b k", b=4),
                                   ACT.Identity, bias=S("bk")).then_inc(a_kT, 1)
                for i in range(4):
                    act.wait_ge(a_vps, 4 * n + i + 1 + START)
                    act.activation(vC[0:KC, 4 * i:4 * i + 4, :, 0:2 * DH].rearrange("p b g v -> p (b g) v"),
                                   PS[0:KC, i, :].rearrange("p (b v) -> p b v", v=2 * DH),
                                   ACT.Copy).then_inc(a_v, 1)
                for u in range(NT):
                    N = NT * n + u
                    act.wait_ge(a_sub, N + 1)
                    act.activation(sS[0:112, u % 2], sS[0:112, u % 2], ACT.Exp).then_inc(a_exp, 1)
                    act.wait_ge(a_max, 3 * N + 3 + START)
                    act.wait_ge(a_am, N - 1 + START)
                    act.activation(alpha[0:112, u % 2], drop[0:112, u % 2], ACT.Exp).then_inc(a_al, 1)
                    for g in range(4):
                        act.wait_ge(a_tp, 4 * N + g + 1 + START)
                        act.wait_ge(a_o, N - 1 + START)
                        act.activation(pT[0:KC, u % 2, 448 * g:448 * g + 448],
                                       PS[0:KC, 4 + (4 * u + g) % 3, 0:448], ACT.Copy).then_inc(a_pT, 1)
            act.wait_ge(a_tps, 1)
            for h in range(2):
                act.activation(oT[:, h].rearrange("p (i b) q -> p i b q", i=4)[:, :, :, 0:NQ],
                               PS[0:64, 0:4, 0:448].rearrange("p i (b h q) -> p i b h q", b=4, h=2)[:, :, :, h, :],
                               ACT.Identity, bias=pair[:, 256 + h:257 + h]).then_inc(a_oT, 1)
            root(4)
            copy_ht(4, 1.0)
            act.wait_ge(r_exp, 3)
            act.activation(ta, lg, ACT.Exp).then_inc(r_exp, 1)
            for m in range(4 * NE):
                act.wait_ge(h_ps, 4 * NE + m + 1)
                if m >= 2:
                    act.wait_ge(h_mul, m - 1)
                act.activation(sil[:, m % 2, 0:448], PS[:, 2 * (m % 3), 0:448], ACT.Silu).then_inc(h_act, 1)

        @block.vector
        def _(dve):
            n_vec = [0]

            def link(ins):
                n_vec[0] += 1
                ins.then_inc(vec, 1)
                dve.wait_ge(vec, n_vec[0])

            s8 = [st8[:, i, :] for i in range(6)]

            def bc(a):
                return a[:, :, None].to_broadcast([128, NT, 128])

            def layernorm(n):
                for t in range(NT):
                    last = dve.bn_stats(bnst[:, t, :], X[:, t, :])
                link(last)
                for t in range(NT):
                    last = dve.bn_aggr(mv[:, t, :], bnst[:, t, :])
                link(last)
                dve.tensor_scalar(s8[2], mv[:, :, 1], EPS, None, ALU.add).then_inc(ln_var, 1)
                dve.wait_ge(ln_std, n)
                link(dve.reciprocal(s8[4], s8[3]))
                for t in range(NT):
                    last = dve.tensor_scalar(H[:, t, :], X[:, t, :], mv[:, t, 0:1], s8[4][:, t:t + 1],
                                             ALU.subtract, ALU.mult)
                last.then_inc(ln_out, 1)

            dve.wait_ge(in_cst, 32)
            dve.wait_ge(in_x, 32)
            dve.wait_ge(pool_init, 2)
            link(dve.tensor_copy(Rv[:, 0, :], C("first")))
            dve.tensor_scalar(mrow[:, 0:1], C("rows")[:, 0:1], 1.0, None, ALU.mult).then_inc(w_row, 1)
            layernorm(1)
            dve.wait_ge(ln_out, 1)
            link(dve.tensor_tensor(SQ[:], H[:], H[:], ALU.mult))
            link(dve.tensor_reduce(s8[5], SQ[:], AX, ALU.add))
            for u in range(NT):
                dve.wait_ge(d_ps, u + 1)
                if u >= 2:
                    for h in range(2):
                        dve.wait_ge(d_put[u % 2][h], 16 * NBLK * (u // 2))
                dve.tensor_scalar(Dt[:, u % 2, :].rearrange("p (i k) -> p i k", i=3),
                                  PS[:, 3 * (u % 2):3 * (u % 2) + 3, 0:CH], s8[5][:, u:u + 1], 0.0,
                                  ALU.add, ALU.max).then_inc(d_add, 1)
            for i in range(2):
                for h in range(2):
                    dve.wait_ge(d_put[i][h], 16 * NBLK * NT // 2)

            def tie(s):
                dve.wait_ge(v_x, s)
                dve.wait_ge(v_z, s)
                dve.scalar_tensor_tensor(over[:, s % RING, :], diag[:, s % RING, :], TINY, over[:, s % RING, :],
                                         ALU.mult, ALU.add).then_inc(v_q, 1)

            def choice(s):
                dve.wait_ge(v_q, s)
                dve.wait_ge(v_f, s)
                dve.scalar_tensor_tensor(Rv[:, s - 1, 1:SW], over[:, s % RING, :], 0.0, Rv[:, s - 1, 1:SW],
                                         ALU.is_gt, ALU.mult).then_inc(v_u, 1)

            for t in range(1, SLOTS):
                if t > 1:
                    dve.wait_ge(w_row, t)
                dve.tensor_tensor(best[:, t % RING, :], Rv[:, t - 1, 1:SW], Rv[:, t - 1, 0:BR], ALU.min).then_inc(w_min, 1)
                if t > 2:
                    tie(t - 2)
                dve.wait_ge(w_min, t)
                if t > 1:
                    dve.wait_ge(w_edge, t - 1)
                dve.tensor_tensor_scan(Rv[:, t, 1:SW], best[:, t % RING, :], Rv[:, t, 1:SW], Rv[:, t, 0:1],
                                       ALU.min, ALU.add).then_inc(w_row, 1)
                if t > 2:
                    choice(t - 2)
            for t in range(SLOTS - 2, SLOTS):
                tie(t)
                choice(t)
            dve.wait_ge(v_put, 16 * puts)

            dve.memset(E[:, 0:1], 0.0)
            link(dve.memset(E[:, NQ:NQ + 1], float(NK - 1)))
            for n in range(NQ - 1):
                if n:
                    dve.wait_ge(b_e, n)
                dve.scalar_tensor_tensor(mrow[:], C("rows"), E[:, NQ - n:NQ - n + 1], C("rows"), ALU.is_le, ALU.mult).then_inc(b_g, 1)
                dve.wait_ge(b_g, n + 1)
                dve.tensor_tensor_reduce(mrow[:], mrow[:], Vcol[:, NQ - 1 - n, :],
                                         1.0, 0.0, ALU.mult, ALU.max, vmax).then_inc(b_max, 1)
                dve.wait_ge(b_max, n + 1)
                dve.tensor_scalar(e8, C("blk"), vmax, None, ALU.mult).then_inc(b_t, 1)
                dve.wait_ge(b_bc, n + 1)
                dve.tensor_reduce(E[:, NQ - 1 - n:NQ - n], PS[:, 1, n * NBLK:(n + 1) * NBLK], AX, ALU.max).then_inc(b_e, 1)
            dve.wait_ge(b_e, NQ - 1)
            dve.tensor_tensor(Ed[0:16, :].rearrange("p (b j) -> p b j", b=NB),
                              E[0:16, None, :].to_broadcast([16, NB, NQ + 1]),
                              C("ident")[0:16, 0:16, None].to_broadcast([16, NB, NQ + 1]), ALU.mult).then_inc(e_tab, 1)
            dve.wait_ge(e_bc, 1)
            W = NB * (NQ + 1) // 2
            link(dve.tensor_copy(Eb[:].rearrange("p (i w) -> p i w", i=2), PS[:, 3:5, 0:W]))
            G1v = G1.rearrange("p (b q) -> p b q", b=NB)
            for c in range(NC):
                i = C("key")[:, c:c + 1]
                link(dve.tensor_scalar(G1v, Ebv[:, :, 1:NQ + 1], i, None, ALU.is_ge))
                dve.scalar_tensor_tensor(Mk[:, c], Ebv[:, :, 0:NQ], C("keyh")[:, c:c + 1], G1v, ALU.is_le, ALU.mult).then_inc(m_ok, 1)
                dve.wait_ge(m_ok, c + 1)
            dve.wait_ge(tanh_ok, 1)
            dve.wait_ge(in_w, 80)
            link(dve.tensor_tensor(wgn[0:8, :], wg_s[:], wg_s[:], ALU.mult))
            dve.tensor_reduce(wgs[0:8, 0:1], wgn[0:8, :], AX, ALU.add).then_inc(wg_sq, 1)
            dve.wait_ge(wg_std, 1)
            link(dve.tensor_scalar(wgs[0:8, 2:3], wgs[0:8, 1:2], 1e-4, None, ALU.max))
            link(dve.reciprocal(wgs[0:8, 3:4], wgs[0:8, 2:3]))
            dve.tensor_scalar(wgn[0:8, :], wg_s[:], wgs[0:8, 3:4], None, ALU.mult).then_inc(wg_r, 1)
            dve.wait_ge(x_ps, 1)
            dve.scalar_tensor_tensor(X[:].rearrange("p t d -> p (t d)").rearrange("p (a w) -> p a w", a=2), PS[:, 5:7, :],
                                     tg[:, 0:1], X[:].rearrange("p t d -> p (t d)").rearrange("p (a w) -> p a w", a=2),
                                     ALU.mult, ALU.add).then_inc(x_up, 1)
            dve.wait_ge(x_up, 1)

            def softmax(n):
                link(dve.tensor_copy(lg, PS[:, 5, 64:128].rearrange("p (t e) -> p t e", t=NT)))
                link(dve.tensor_reduce(s8[0], lg, AX, ALU.max))
                dve.tensor_tensor(lg, lg, s8[0][:, :, None].to_broadcast([128, NT, NE]), ALU.subtract).then_inc(r_exp, 1)
                dve.wait_ge(r_exp, n)
                link(dve.tensor_reduce(s8[0], ta, AX, ALU.add))
                link(dve.reciprocal(s8[1], s8[0]))
                link(dve.tensor_tensor(ta, ta, s8[1][:, :, None].to_broadcast([128, NT, NE]), ALU.mult))

            def first_of(dst, src, w, m):
                tmp = td[:, :, 0:w]
                rank = C("rank8" if w == 8 else "rank4")[:, None, 0:w].to_broadcast([128, NT, w])
                link(dve.tensor_reduce(m, src, AX, ALU.max))
                link(dve.tensor_tensor(dst, src, m[:, :, None].to_broadcast([128, NT, w]), ALU.is_equal))
                link(dve.tensor_tensor(dst, dst, rank, ALU.mult))
                link(dve.tensor_reduce(s8[5], dst, AX, ALU.max))
                link(dve.tensor_tensor(dst, dst, s8[5][:, :, None].to_broadcast([128, NT, w]), ALU.is_equal))

            def experts_add(base, i):
                e, th = i // 2, i % 2
                dve.wait_ge(o_ps, base + i + 1)
                for t in range(4):
                    ins = dve.scalar_tensor_tensor(X[:, 4 * th + t, :], PS[:, 6 + th, 128 * t:128 * t + 128],
                                                   cf[:, 4 * th + t, e:e + 1], X[:, 4 * th + t, :], ALU.mult, ALU.add)
                ins.then_inc(o_add, 1)
                dve.wait_ge(o_add, base + i + 1)

            Xh = X[:].rearrange("p t d -> p (t d)").rearrange("p (a w) -> p a w", a=2)

            layernorm(2)
            dve.wait_ge(lg_ps, 2)
            softmax(2)
            first_of(cf, ta, NE, s8[2])
            link(dve.tensor_tensor(cf, cf, s8[2][:, :, None].to_broadcast([128, NT, NE]), ALU.mult))
            dve.tensor_scalar(cf, cf, tg[:, 2:3], None, ALU.mult).then_inc(r_max, 1)
            dve.wait_ge(r_max, 1)
            for i in range(2 * NE):
                experts_add(0, i)
                if i == 7:
                    dve.wait_ge(b2_ok, 2)
                    link(dve.tensor_tensor(Xh, Xh, PS[:, 4:6, :], ALU.add))

            dve.wait_ge(in_mask, 32)
            link(dve.tensor_copy(capA[0:112], msk8[0:112]))
            link(dve.tensor_scalar(capB[0:112], capA[0:112], 0.5, None, ALU.is_lt))
            link(dve.tensor_reduce(sm[0:56, 576:588], capB[0:56].rearrange("p (c k) -> p c k", c=NC), AX, ALU.max))
            link(dve.tensor_reduce(sm[0:56, 588:589], sm[0:56, 576:588], AX, ALU.max))
            link(dve.tensor_scalar(sm[0:56, 588:589], sm[0:56, 588:589], 0.5, None, ALU.is_lt))
            link(dve.tensor_scalar(capA[0:112], capA[0:112], -1e9, None, ALU.mult))
            dve.scalar_tensor_tensor(cap[0:112], capB[0:112], MAXV, capA[0:112], ALU.mult, ALU.add).then_inc(cap_ok, 1)
            dve.wait_ge(live_t, 1)
            dve.tensor_reduce(sm[0:13, 592:593], PS[0:13, 0, 0:56], AX, ALU.max).then_inc(live_f, 1)
            dve.wait_ge(live_t, 2)
            link(dve.tensor_tensor(sm[0:1, 596:609], PS[0:1, 0, 64:77], C("late")[0:1, 0:13], ALU.mult))
            link(dve.tensor_reduce(sm[0:1, 612:613], sm[0:1, 596:609], AX, ALU.max))
            dve.tensor_copy(live_i[0:1, 0:1], sm[0:1, 612:613]).then_inc(live_ok, 1)
            dve.wait_ge(live_ok, 1)
            layernorm(3)
            dve.wait_ge(q_ps, 1)
            for i in range(2):
                q = PS[:, i, :].rearrange("p (b q) -> p b q", b=8)[:, :, 0:NQ]
                for h in range(4):
                    last = dve.tensor_scalar(qbd[:, 8 * i:8 * i + 8, h, :], q, S("bq"), C("sel")[:, h:h + 1],
                                             ALU.add, ALU.mult)
            last.then_inc(q_sb, 1)
            live = dve.value_load(live_i[0:1, 0:1], min_val=1, max_val=NC)

            def accumulate(N, u):
                a = acc[0:112, u]
                dve.wait_ge(a_al, N + 1)
                dve.wait_ge(a_acc, N + START)
                dve.tensor_tensor(a, a, alpha[0:112, u % 2, :, None].to_broadcast([112, 16, VW]), ALU.mult).then_inc(a_am, 1)
                dve.wait_ge(a_am, N + 1 + START)
                dve.wait_ge(a_o, N + 1 + START)
                dve.tensor_tensor(a, a, PS[0:112, 7, 0:16 * VW].rearrange("p (g v) -> p g v", v=VW), ALU.add).then_inc(a_acc, 1)

            with dve.Fori(0, live) as n:
                key = dve.snap(n * -KC + (NC - 1) * KC)
                k = cap[0:112, bass.ds(key, KC)]
                for u in range(NT):
                    N = NT * n + u
                    S2 = sS[0:112, u % 2]
                    dve.wait_ge(a_s, N + 1)
                    dve.wait_ge(a_tp, 4 * N - 4 + START)
                    dve.tensor_tensor(S2.rearrange("p (g r) k -> p g r k", g=4),
                                      PS[0:112, 0:4, 0:CH].rearrange("p g (r k) -> p g r k", k=KC),
                                      k[:, None, None, :].to_broadcast([112, 4, 4, KC]), ALU.min).then_inc(a_min, 1)
                    dve.wait_ge(a_min, N + 1 + START)
                    dve.tensor_reduce(mtmp[0:112, u % 2], S2, AX, ALU.max).then_inc(a_max, 1)
                    dve.wait_ge(a_max, 3 * N + 1 + START)
                    dve.wait_ge(a_mr, N - 1 + START)
                    dve.tensor_tensor(mnew[0:112, u % 2], mtmp[0:112, u % 2], mrun[0:112, u], ALU.max).then_inc(a_max, 1)
                    dve.wait_ge(a_max, 3 * N + 2 + START)
                    dve.tensor_tensor(drop[0:112, u % 2], mrun[0:112, u], mnew[0:112, u % 2], ALU.subtract).then_inc(a_max, 1)
                    if u:
                        accumulate(N - 1, u - 1)
                accumulate(NT * n + NT - 1, NT - 1)
            dve.wait_ge(a_acc, live * NT + START)
            dve.wait_ge(a_mr, live * NT + START)
            link(dve.reciprocal(mrun[0:112], acc[0:112, :, :, VW - 1]))
            a = acc[0:112].rearrange("p u (g h) v -> p (u g) h v", h=2)
            rc = mrun[0:112].rearrange("p u (g h) -> p (u g) h", h=2)
            for h in range(2):
                o = oN[0:112, h]
                link(dve.tensor_scalar(o, a[:, :, h, 0:DH], C("half")[0:112, 0:1], None, ALU.mult))
                link(dve.scalar_tensor_tensor(o, a[:, :, h, DH:2 * DH], C("half")[0:112, 1:2], o, ALU.mult, ALU.add))
                last = dve.tensor_tensor(o, o, rc[:, :, h, None].to_broadcast([112, 64, DH]), ALU.mult)
            last.then_inc(a_fin, 1)
            dve.wait_ge(wo_ps, 1)
            dve.scalar_tensor_tensor(Xh, PS[:, 4:6, :], tg[:, 1:2], Xh, ALU.mult, ALU.add).then_inc(x_up, 1)
            dve.wait_ge(x_up, 2)

            layernorm(4)
            dve.wait_ge(lg_ps, 3)
            softmax(4)
            grp, oh = tb[:, :, 0:4], tc[:, :, 0:4]
            pair = ta.rearrange("p t (g i) -> p t g i", i=2)
            link(dve.tensor_tensor(grp, pair[:, :, :, 0], pair[:, :, :, 1], ALU.max))
            first_of(oh, grp, 4, s8[2])
            link(dve.scalar_tensor_tensor(grp, oh, -2.0, grp, ALU.mult, ALU.add))
            o2 = tb[:, :, 4:8]
            first_of(o2, grp, 4, s8[2])
            link(dve.tensor_tensor(oh, oh, o2, ALU.add))
            link(dve.tensor_tensor(pair, pair, oh[:, :, :, None].to_broadcast([128, NT, 4, 2]), ALU.mult))
            first_of(tb, ta, NE, s8[2])
            link(dve.scalar_tensor_tensor(cf, tb, -2.0, ta, ALU.mult, ALU.add))
            first_of(tc, cf, NE, s8[3])
            link(dve.tensor_tensor(s8[2], s8[2], s8[3], ALU.add))
            link(dve.reciprocal(s8[3], s8[2]))
            link(dve.tensor_tensor(tb, tb, tc, ALU.add))
            link(dve.tensor_tensor(cf, tb, ta, ALU.mult))
            link(dve.tensor_tensor(cf, cf, s8[3][:, :, None].to_broadcast([128, NT, NE]), ALU.mult))
            dve.tensor_scalar(cf, cf, tg[:, 3:4], None, ALU.mult).then_inc(r_max, 1)
            dve.wait_ge(r_max, 2)
            for m in range(4 * NE):
                i, a = m // 2, m % 2
                dve.wait_ge(h_act, 4 * NE + m + 1)
                if i >= 3:
                    dve.wait_ge(o_ps, 2 * NE + i - 2)
                dve.tensor_tensor(gT[:, i % 3, a, :].rearrange("p (b q) -> p b q", q=64)[:, :, 0:NQ],
                                  sil[:, m % 2, 0:448].rearrange("p (b q) -> p b q", q=NQ),
                                  PS[:, 2 * (m % 3) + 1, 0:448].rearrange("p (b q) -> p b q", q=NQ), ALU.mult).then_inc(h_mul, 1)
                if a and i:
                    experts_add(2 * NE, i - 1)
            experts_add(2 * NE, 2 * NE - 1)


def kernel(**inputs):
    import concourse.bacc as _bacc
    from concourse.bass_utils import run_bass_kernel_spmd as _run

    a = {k: np.asarray(v) for k, v in inputs.items()}
    ctx = np.ascontiguousarray(a["ctx_1024"])
    parts = {"wq": a["L1_xattn_W_q"], "wk": a["L1_xattn_W_k"], "wv": a["L1_xattn_W_v"],
             "wred": a["L0_ffn_w_red"], "gate": a["L1_ffn_gate_w"].T, "bq": a["L1_xattn_b_q"][:, None],
             "bk": a["L1_xattn_b_k"][:, None],
             "b1": a["L0_ffn_b1"].reshape(2 * NE, 128).T,
             "g": np.broadcast_to(np.concatenate([a["g_xattn"], a["g_ffn"]])[None, :], (128, 4))}
    b2 = np.zeros((NT, NE, NT, 128), np.float32)
    for t in range(NT):
        b2[t, :, t] = a["L0_ffn_b2"]
    b2 = b2.reshape(NT * NE, NT * 128)
    arrays = {
        "x": a["x"],
        "ctx": ctx,
        "ctxT": ctx.transpose(0, 2, 1),
        "mask": a["mask_1x1xSxS2_bk1"].reshape(NQ, NK),
        "cst": const_values(),
        "small": np.concatenate([parts[n] for n, _ in SMALL], axis=1),
        "bo": a["L1_xattn_b_o"][None, :],
        "wg": a["L0_ffn_wg"],
        "pair": np.concatenate([a["L1_xattn_W_o"].reshape(8, 2, DH, 128).transpose(0, 2, 1, 3).reshape(64, 256),
                                a["L1_xattn_b_v"].reshape(8, 2, DH).transpose(0, 2, 1).reshape(64, 2)], axis=1),
        "b2": b2,
        "w1": a["L0_ffn_W1"],
        "w2": a["L0_ffn_W2"].reshape(2 * NE, 128, 128).transpose(1, 0, 2),
        "w13": a["L1_ffn_w13_weight"].transpose(2, 0, 1),
        "w2b": a["L1_ffn_w2_weight"].transpose(0, 2, 1).reshape(2 * NE, 128, 128).transpose(1, 0, 2),
    }
    nc = _bacc.Bacc("TRN2", target_bir_lowering=False, num_devices=1)
    fed, args = {}, []
    for name, v in arrays.items():
        v = np.ascontiguousarray(v)
        fed[f"in_{name}"] = v
        args.append(nc.dram_tensor(f"in_{name}", v.shape, mybir.dt.from_np(v.dtype), kind="ExternalInput").ap())
    out = nc.dram_tensor("out_0", (NB, NQ, ND), F32, kind="ExternalOutput").ap()
    flamingo(nc, *args, out)
    r = _run(nc, [fed], core_ids=[0])
    return r.results[0]["out_0"]
```

```python
from contextlib import ExitStack

import numpy as np
import concourse.bass as bass
from concourse import mybir

ALU = mybir.AluOpType
ACT = mybir.ActivationFunctionType
F32 = mybir.dt.float32
I32 = mybir.dt.int32
U8 = mybir.dt.uint8
AX = mybir.AxisListType.X

NB, NQ, ND, NK = 16, 56, 128, 1500
NT = NB // 2
NE = 8
NH, DH = 16, 8
BIG = 1e30
NBLK = 8
BR = -(-NK // NBLK)
LAG = 2
SLOTS = 1 + NQ + LAG * (NBLK - 1)
SW = BR + 1
VG = 7
RING = 4
DIAG = 2.0 ** -12
STEEP = 2.0 ** 13
TINY = 1e-30
KC, NC = 125, 12
CH = 500
MAXV = 3e38
EPS = 1e-5


def const_layout():
    names = [("ident", 128), ("shift", 128), ("same", 32), ("ones", 128), ("rows", BR), ("edge", 1),
             ("first", SW), ("sel", 4), ("rank8", 8), ("rank4", 8), ("late", 16), ("own", NB), ("half", 2), ("zero", 128),
             ("tiny", 1), ("keyh", NC), ("end", NC)]
    at, out = 0, {}
    for n, w in names:
        out[n] = (at, w)
        at += w
    return out, at


def const_values():
    lay, width = const_layout()
    c = np.zeros((128, width), np.float32)
    p = np.arange(128)

    def put(name, v):
        a, w = lay[name]
        c[:, a:a + w] = v

    put("ident", np.eye(128))
    put("shift", (p[None, :] == p[:, None] + 1) & (p[None, :] % NBLK > 0))
    put("same", np.arange(32)[None, :] // NBLK == (p[:, None] % 32) // NBLK)
    put("ones", 1.0)
    put("rows", BR * (p[:, None] % NBLK) + np.arange(BR)[None, :])
    put("edge", np.where(p[:, None] % NBLK == 0, BIG, 0.0))
    first = np.full((128, SW), BIG)
    first[::NBLK, 0] = 0.0
    put("first", first)
    inh = (p[:, None] % 32) // DH == np.arange(4)[None, :]
    put("sel", inh / np.sqrt(np.float32(DH)))
    put("half", np.stack([p < NQ, p >= NQ], 1))
    put("keyh", NC * p[:, None] + np.arange(NC)[None, :] + 0.5)
    put("end", 1.0 - STEEP * (NC * p[:, None] + np.arange(NC)[None, :]))
    put("tiny", TINY)
    put("rank8", NE - np.arange(8))
    put("rank4", np.r_[4 - np.arange(4), np.zeros(4)])
    put("own", p[:, None] == NBLK * np.arange(NB)[None, :])
    put("late", np.r_[NC - np.arange(NC), NC, np.zeros(3)])
    return c


SMALL = [("wq", 128), ("wk", 128), ("wv", 128), ("wred", 16), ("gate", 8), ("bq", 1), ("bk", 1),
         ("b1", 16), ("g", 4)]
VW = 2 * DH + 1


def small_layout():
    at, out = 0, {}
    for n, w in SMALL:
        out[n] = (at, w)
        at += w
    return out, at


def flamingo(nc, x, ctx, ctxT, mask, cst_h, small_h, bo_h, wg, pair_h, b2_h, w1, w2, w13, w2b, out):
    st = ExitStack()
    clay, cw = const_layout()
    slay, sw = small_layout()
    with st:
        def sb(name, shape, dt=F32):
            return st.enter_context(nc.sbuf_tensor(name, shape, dt))

        def sem(name):
            return st.enter_context(nc.semaphore(name))

        cst = sb("cst", [128, cw])
        small = sb("small", [128, sw])
        bo = sb("bo", [1, 128])
        pair = sb("pair", [128, 130])
        wg_s = sb("wg_s", [NE, 16])
        kT = sb("kT", [128, NB, KC])
        vC = sb("vC", [128, NB, 8, VW])
        X = sb("X", [128, NT, 128])
        HS = sb("HS", [128, 2 * NT * 128])
        HT = sb("HT", [128, NT, 128])
        st8 = sb("st8", [128, 6, NT])
        R = sb("R", [128, SLOTS * SW])
        VM = sb("VM", [128, NC * NB * 56])
        CA = sb("CA", [128, 8 * NC * 128])
        best = sb("best", [128, RING, BR])
        diag = sb("diag", [128, RING, BR])
        over = sb("over", [128, RING, BR])
        leaving = sb("leaving", [128, BR])
        sm = sb("sm", [128, 640])
        live_i = sb("live_i", [1, 4], I32)
        PS = st.enter_context(nc.psum_tensor("PS", [128, 8, 512], F32))

        H = HS[:, 0:NT * 128].rearrange("p (t d) -> p t d", t=NT)
        SQ = HS[:, NT * 128:2 * NT * 128].rearrange("p (t d) -> p t d", t=NT)
        ckT = HS[:, 0:NB * KC].rearrange("p (b k) -> p b k", b=NB)

        def C(n):
            a, w = clay[n]
            return cst[:, a:a + w]

        def S(n):
            a, w = slay[n]
            return small[:, a:a + w]

        def small_area(a, w):
            return sm[:, a:a + w]

        Rv = R[:].rearrange("p (t c) -> p t c", c=SW)
        Vcol = VM[:, 0:NQ * BR].rearrange("p (j r) -> p j r", r=BR)
        Mk = VM[:].rearrange("p (c b q) -> p c b q", c=NC, b=NB)
        cT = CA[:, 0:6000].rearrange("p (n k) -> p n k", n=4)
        cSq = CA[:, 6000:9000].rearrange("p (n k) -> p n k", n=2)
        Dt = CA[:, 9000:12000].rearrange("p (n k) -> p n k", n=2)
        nat = [CA[:, 0:8 * NC * 128].rearrange("p (b c d) -> p b c d", b=8, c=NC),
               R[:, 0:8 * NC * 128].rearrange("p (b c d) -> p b c d", b=8, c=NC)]
        gT = CA[:, 0:3072].rearrange("p (n a t) -> p n a t", n=3, a=2)
        sil = CA[:, 3072:4096].rearrange("p (n t) -> p n t", n=2)
        b2d = CA[0:64, 4096:5120]
        cfT = CA[0:64, 5120:5248]
        acc = R[:, 0:NT * 16 * VW].rearrange("p (u g v) -> p u g v", u=NT, g=16)
        pT = R[:, 2176:2176 + 2 * 1792].rearrange("p (n k) -> p n k", n=2)
        qbd = R[:, 7168:7168 + NB * 4 * NQ].rearrange("p (b h q) -> p b h q", b=NB, h=4)
        oN = R[:, 5760:5760 + 1024].rearrange("p (h g d) -> p h g d", h=2, d=DH)
        cap = R[:, 10752:12252]
        avT = R[:, 12252:12252 + 448]
        W1 = CA[:, 5248:7296].rearrange("p (e i) -> p e i", e=NE)
        W2 = CA[:, 7296:9344].rearrange("p (e i) -> p e i", e=2 * NE)
        sS = CA[:, 0:4000].rearrange("p (n g k) -> p n g k", n=2, g=16)
        W13 = VM[:, 0:4096].rearrange("p (e i) -> p e i", e=NE)
        W2B = VM[:, 4096:6144].rearrange("p (e i) -> p e i", e=2 * NE)
        oT = VM[:, 6144:6144 + 1024].rearrange("p (b q) -> p b q", b=NB)
        msk8 = CA[:, 10844:11219].bitcast(U8)
        capA = CA[:, 9344:10844]
        capB = VM[:, 9000:10500]

        tg = small_area(0, 4)
        E = small_area(8, NQ + 1)
        block_max = sb("block_max", [128, 1])
        blocks = sb("blocks", [128, 32])
        wgn = small_area(96, 16)
        wgs = small_area(112, 4)
        wgT = small_area(116, 8)
        lg = small_area(128, 64).rearrange("p (t e) -> p t e", t=NT)
        cf = small_area(192, 64).rearrange("p (t e) -> p t e", t=NT)
        ta = small_area(256, 64).rearrange("p (t e) -> p t e", t=NT)
        tb = small_area(320, 64).rearrange("p (t e) -> p t e", t=NT)
        tc = small_area(384, 64).rearrange("p (t e) -> p t e", t=NT)
        td = small_area(448, 64).rearrange("p (t e) -> p t e", t=NT)
        mrun = sb("mrun", [128, NT, 16])
        mtmp = sb("mtmp", [128, 2, 16])
        mnew = sb("mnew", [128, 2, 16])
        drop = sb("drop", [128, 2, 16])
        alpha = sb("alpha", [128, 4, 16])
        bnst = sb("bnst", [128, NT, 6])
        mv = sb("mv", [128, NT, 2])
        Eb = sb("Eb", [128, NB * (NQ + 1)])
        Ed = HS[:, NT * 128:NT * 128 + NB * (NQ + 1)]
        G1v = HS[:, 0:2 * NB * NQ].rearrange("p (n b q) -> p n b q", n=2, b=NB)
        Ebv = Eb[:].rearrange("p (b j) -> p b j", b=NB)

        in_cst = sem("in_cst")
        in_x = sem("in_x")
        in_w = sem("in_w")
        in_ct = [sem(f"in_ct{i}") for i in range(4)]
        in_nat = sem("in_nat")
        in_nat2 = sem("in_nat2")
        in_w1 = sem("in_w1")
        in_w13 = sem("in_w13")
        in_mask = sem("in_mask")
        vec = sem("vec_step")
        pool_init = sem("pool_init")
        ln_var = sem("ln_var")
        ln_std = sem("ln_std")
        ln_out = sem("ln_out")
        ht_ps = sem("ht_ps")
        ht_sb = sem("ht_sb")
        sq_ok = sem("ctx_squared")
        d_half = sem("dist_psum")
        d_add = sem("dist_added")
        d_root = sem("dist_root")
        d_put = [[sem(f"dist_placed{i}_{h}") for h in range(2)] for i in range(2)]
        w_min = sem("wave_min")
        w_row = sem("wave_row")
        w_shift = sem("wave_shifted")
        w_edge = sem("wave_edge")
        v_y = sem("choice_left_over")
        v_z = sem("choice_diagonal")
        v_x = sem("choice_difference")
        v_f = sem("choice_factor")
        v_q = sem("choice_tie")
        v_u = sem("choice_made")
        v_put = sem("choice_placed")
        b_g = sem("back_mask")
        b_max = sem("back_blockmax")
        b_t = sem("back_transposed")
        b_e = sem("back_max")
        e_tab = sem("e_diag")
        e_bc = sem("e_broadcast")
        m_ok = sem("path_mask")
        m_end = sem("path_end")
        x_ps = sem("aligned_psum")
        x_up = sem("x_updated")
        wg_t = sem("router_transposed")
        wg_r = sem("router_ready")
        wg_sq = sem("router_squares")
        wg_std = sem("router_norms")
        lg_ps = sem("logits_psum")
        lg_cp = sem("logits_copied")
        lg_rd = sem("router_reduced")
        r_max = sem("route_max")
        r_exp = sem("route_exp")
        h_ps = sem("hidden_psum")
        h_act = sem("hidden_act")
        h_mul = sem("hidden_mul")
        o_ps = sem("expert_psum")
        o_add = sem("expert_added")
        tanh_ok = sem("gates_tanh")
        q_ps = sem("query_psum")
        q_sb = sem("query_blocks")
        cap_ok = sem("mask_cap")
        live_t = sem("live_psum")
        live_f = sem("live_flags")
        live_ok = sem("live_chunks")
        a_in = sem("attn_ctx_in")
        a_kps = sem("attn_k_psum")
        a_kT = sem("attn_k")
        a_vps = sem("attn_v_psum")
        a_v = sem("attn_v")
        a_s = sem("attn_scores")
        a_min = sem("attn_capped")
        a_max = sem("attn_max")
        a_mr = sem("attn_running_max")
        a_sub = sem("attn_shifted")
        a_al = sem("attn_rescale")
        a_am = sem("attn_rescaled")
        a_tps = sem("attn_out_transposed")
        a_oT = sem("attn_out_T")
        a_oT2 = sem("attn_out_T2")
        pool_late = sem("pool_late")
        b2_ok = sem("bias_psum")
        b2_t = sem("bias_coeff_T")
        in_b2 = sem("in_b2")
        a_exp = sem("attn_exp")
        a_tp = sem("attn_p_transposed")
        a_pT = sem("attn_pT")
        a_o = sem("attn_out_psum")
        a_os = sem("attn_out_copied")
        a_bk = sem("attn_out_turned")
        a_acc = sem("attn_accumulated")
        bo_ps = sem("out_bias_psum")
        a_fin = sem("attn_norm")
        wo_ps = sem("attn_projected")
        out_s = sem("out_stored")

        block = st.enter_context(nc.Block())

        def first(n):
            return isinstance(n, int)

        more = [1] * (NT - 1) + [3]
        by_sync = [[(0, k) for k in range(NBLK)] + [(1, k) for k in range(m)] for m in more]
        by_pool = [[(1, k) for k in range(m, NBLK)] for m in more]

        def place(eng, u, h, k):
            n, p = min(BR, NK - BR * k), NBLK * (2 * u + h) + k
            return eng.dma_start(Rv[p:p + 1, 1 + LAG * k:1 + LAG * k + NQ, 1:1 + n],
                                 Dt[64 * h:64 * h + NQ, u % 2, BR * k:BR * k + n])

        def outputs(half, h):
            return PS[0:64, 2 * half:2 * half + 2, 0:448].rearrange("p i (b h q) -> p i b h q", b=4, h=2)[:, :, :, h, :]

        def outputs_T(half, h):
            return oT[64 * h:64 * h + 64, 8 * half:8 * half + 8, :].rearrange("p (i b) q -> p i b q", i=2)[:, :, :, 0:NQ]

        def turned_bank(n, a):
            return 7 - a if n == 2 else 6 + a

        keys_T = ctxT.rearrange("b d k -> d b k")

        def columns_of(t0, t1):
            for k in range(NBLK):
                a = max(t0, 2 + LAG * k)
                b = min(t1, NQ + 1 + LAG * k)
                if a < b:
                    yield k, a - 1, b - a, a - 1 - LAG * k
        groups = [(a, min(a + VG, SLOTS)) for a in range(1, SLOTS, VG)]
        puts = sum(sum(1 for _ in columns_of(*g)) for g in groups)

        @block.sync
        def _(sp):
            sp.dma_start(cst[:], cst_h).then_inc(in_cst, 16)
            xs = x.rearrange("(t h) q d -> h q t d", h=2)
            sp.wait_ge(pool_init, 1)
            sp.dma_start(X[0:NQ, :, :], xs[0]).then_inc(in_x, 16)
            sp.dma_start(X[64:64 + NQ, :, :], xs[1]).then_inc(in_x, 16)
            sp.dma_start(small[:], small_h).then_inc(in_cst, 16)
            for b in range(4):
                sp.dma_start(cT[:, b, :], ctxT[b]).then_inc(in_ct[b], 16)
            sp.dma_start(bo[:], bo_h).then_inc(in_w, 16)
            sp.dma_start(wg_s[:], wg).then_inc(in_w, 16)
            sp.dma_start(pair[:], pair_h).then_inc(in_w, 16)
            for u in range(NT):
                for b in (2 * u + 4, 2 * u + 5):
                    if b < NB:
                        sp.wait_ge(d_half, b - 3)
                        sp.dma_start(cT[:, b % 4, :], ctxT[b]).then_inc(in_ct[b % 4], 16)
                sp.wait_ge(d_root, u + 1)
                if u == 0:
                    sp.wait_ge(pool_init, 2)
                for h, k in by_sync[u]:
                    place(sp, u, h, k).then_inc(d_put[u % 2][0], 16)
            for i in range(2):
                sp.wait_ge(d_put[i][0], 16 * sum(map(len, by_sync[i::2])))
                sp.wait_ge(d_put[i][1], 16 * sum(map(len, by_pool[i::2])))
            sp.dma_start(nat[0][0:KC], ctx.rearrange("b (p c) d -> p b c d", c=NC)[:, 0:8]).then_inc(in_nat, 16)
            for t0, t1 in groups:
                sp.wait_ge(v_u, t1 - 1)
                for k, a, n, j in columns_of(t0, t1):
                    sp.dma_start(Vcol[k::NBLK, j:j + n, :],
                                 Rv[k::NBLK, a:a + n, 1:SW]).then_inc(v_put, 16)
            sp.wait_ge(v_put, 16 * puts)
            sp.dma_start(ckT, keys_T[:, :, (NC - 1) * KC:NK]).then_inc(a_in, 16)
            sp.dma_start(nat[1][0:KC], ctx.rearrange("b (p c) d -> p b c d", c=NC)[:, 8:16]).then_inc(in_nat2, 16)
            sp.wait_ge(x_ps, 2)
            sp.dma_start(W1, w1.rearrange("e c h -> c e h")).then_inc(in_w1, 16)
            sp.dma_start(W2, w2).then_inc(in_w1, 16)
            sp.dma_start(b2d, b2_h).then_inc(in_b2, 16)
            for h in range(2):
                sp.dma_start(msk8[NQ * h:NQ * h + NQ, :], mask).then_inc(in_mask, 16)
            sp.dma_start(W13, w13).then_inc(in_w13, 16)
            sp.dma_start(W2B, w2b).then_inc(in_w13, 16)
            sp.wait_ge(live_ok, 1)
            live = sp.value_load(live_i[0:1, 0:1], min_val=1, max_val=NC)
            sp.wait_ge(q_ps, 2)
            with sp.If(live > 1):
                with sp.Fori(1, live) as n:
                    key = sp.snap(n * -KC + (NC - 1) * KC)
                    sp.wait_ge(a_vps, 4 * n)
                    sp.dma_start(ckT, keys_T[:, :, bass.ds(key, KC)]).then_inc(a_in, 16)
            sp.wait_ge(o_add, 4 * NE)
            os = out.rearrange("(t h) q d -> h q t d", h=2)
            sp.dma_start(os[0], X[0:NQ, :, :]).then_inc(out_s, 16)
            sp.dma_start(os[1], X[64:64 + NQ, :, :]).then_inc(out_s, 16)
            sp.wait_ge(out_s, 32)

        @block.gpsimd
        def _(pool):
            pool.memset(X[:], 0.0).then_inc(pool_init, 1)
            pool.memset(R[:], BIG).then_inc(pool_init, 1)
            pool.memset(vC[:], 1.0).then_inc(pool_init, 1)
            pool.wait_ge(pool_init, 3)
            for u in range(NT):
                pool.wait_ge(d_root, u + 1)
                for h, k in by_pool[u]:
                    place(pool, u, h, k).then_inc(d_put[u % 2][1], 16)
            for t in range(1, SLOTS):
                pool.wait_ge(w_row, t)
                if t > RING:
                    pool.wait_ge(v_u, t - RING)
                pool.tensor_tensor(diag[:, t % RING, :], Rv[:, t - 1, 1:SW], Rv[:, t - 1, 0:BR], ALU.subtract).then_inc(v_y, 1)
                pool.wait_ge(w_row, t + 1)
                pool.tensor_tensor(over[:, t % RING, :], Rv[:, t, 0:BR], best[:, t % RING, :], ALU.subtract).then_inc(v_x, 1)
            pool.wait_ge(x_ps, 2)
            pool.memset(gT.rearrange("p n a (b q) -> p (n a b) q", q=64)[:, :, NQ:64], 0.0)
            pool.memset(acc, 0.0)
            pool.memset(oT, 0.0)
            pool.memset(mrun[:], -MAXV).then_inc(pool_late, 1)
            pool.wait_ge(live_ok, 1)
            live = pool.value_load(live_i[0:1, 0:1], min_val=1, max_val=NC)

            def chunk(n):
                for u in range(NT):
                    pool.wait_ge(a_max, 3 * NT * n + 3 * u + 2)
                    pool.tensor_tensor(sS[0:112, u % 2], sS[0:112, u % 2],
                                       mnew[0:112, u % 2, :, None].to_broadcast([112, 16, KC]),
                                       ALU.subtract).then_inc(a_sub, 1)
                    pool.wait_ge(a_max, 3 * NT * n + 3 * u + 3)
                    pool.tensor_tensor(mrun[0:112, u, :], mnew[0:112, u % 2, :], C("ones")[0:112, 0:16], ALU.mult).then_inc(a_mr, 1)

            chunk(0)
            with pool.If(live > 1):
                with pool.Fori(1, live) as n:
                    chunk(n)

        @block.tensor
        def _(pe):
            ident = C("ident")

            def project(n):
                pe.wait_ge(a_in, 16 * n + 16)
                for i in range(4):
                    last = pe.matmul(PS[:, i, 0:CH], S("wk"), ckT[:, 4 * i:4 * i + 4, :], start=True, stop=True)
                last.then_inc(a_kps, 1)
                for i in range(4):
                    pe.wait_ge(a_kT, 4 * n + i + 1)
                    for b in range(4):
                        last = pe.matmul(PS[0:KC, i, 128 * b:128 * b + 128], ckT[:, 4 * i + b, :], S("wv"),
                                         start=True, stop=True)
                    last.then_inc(a_vps, 1)

            def transposes(n, a):
                pe.wait_ge(ln_out, 2 * n - 1 + a)
                for t in range(4):
                    last = pe.transpose(PS[:, turned_bank(n, a), 128 * t:128 * t + 128], H[:, 4 * a + t, :], ident)
                last.then_inc(ht_ps, 1)

            pe.wait_ge(in_cst, 32)
            def squares(b):
                pe.wait_ge(sq_ok, b + 1)
                for i in range(3):
                    pe.matmul(PS[64 * (b % 2):64 * (b % 2) + 64, 3 * (b // 2 % 2) + i, 0:CH], C("ones")[:, 0:64],
                              cSq[:, b % 2, CH * i:CH * i + CH], start=True, stop=False)

            def crossed(b):
                pe.wait_ge(in_ct[b % 4], 16 * (b // 4 + 1))
                for i in range(3):
                    last = pe.matmul(PS[64 * (b % 2):64 * (b % 2) + 64, 3 * (b // 2 % 2) + i, 0:CH],
                                     HT[:, b // 2, 64 * (b % 2):64 * (b % 2) + 64], cT[:, b % 4, CH * i:CH * i + CH],
                                     start=False, stop=True)
                last.then_inc(d_half, 1)

            squares(0)
            transposes(1, 0)
            transposes(1, 1)
            for b in range(NB):
                if b:
                    if b % 2 == 0 and b >= 4:
                        pe.wait_ge(d_add, b // 2 - 1)
                    squares(b)
                if b == 0:
                    pe.wait_ge(ht_sb, 1)
                if b == NB // 2:
                    pe.wait_ge(ht_sb, 2)
                crossed(b)
            pe.wait_ge(d_add, NT)
            for t in range(SLOTS - 2):
                pe.wait_ge(w_row, t + 1)
                if t:
                    pe.wait_ge(w_edge, t)
                pe.matmul(PS[:, 0, t:t + 1], C("shift"), Rv[:, t, BR:BR + 1], start=True, stop=True).then_inc(w_shift, 1)
            pe.wait_ge(w_edge, SLOTS - 2)
            project(0)
            pe.wait_ge(e_tab, 1)
            pe.wait_ge(a_v, 4)
            W = NB * (NQ + 1) // 2
            for i in range(2):
                last = pe.matmul(PS[:, 3 + i, 0:W], C("ones"), Ed[:, W * i:W * i + W],
                                 start=True, stop=True)
            last.then_inc(e_bc, 1)
            for i in range(2):
                pe.matmul(PS[:, 5 + i, :], C("zero")[0:1, :], C("ones")[0:1, 0:1].to_broadcast([1, 512]), start=True, stop=False,
                          skip_group_check=True)
            pe.wait_ge(in_nat, 16)
            pe.wait_ge(in_nat2, 16)
            def path_sums(c, half):
                pe.wait_ge(m_ok, c + 1)
                for b in range(8 * half, 8 * half + 8):
                    t, h = b // 2, b % 2
                    last = pe.matmul(PS[64 * h:64 * h + NQ, 5 + half, 128 * (t % 4):128 * (t % 4) + 128],
                                     Mk[0:KC, c, b, :], nat[half][0:KC, b % 8, c, :],
                                     start=False, stop=(c == NC - 1), skip_group_check=True)
                return last

            for c in range(NC // 2):
                path_sums(c, 0)
                path_sums(c, 1)
            for c in range(NC // 2, NC):
                last = path_sums(c, 0)
            last.then_inc(x_ps, 1)
            pe.wait_ge(wg_r, 1)
            pe.transpose(PS[0:16, 3, 0:8], wgn[0:8, :], C("ident")[0:8, 0:8]).then_inc(wg_t, 1)
            for c in range(NC // 2, NC):
                last = path_sums(c, 1)
            last.then_inc(x_ps, 1)

            def tokens(th):
                return HT[:, 4 * th:4 * th + 4, :].rearrange("p t (h q) -> p (t h) q", h=2)[:, :, 0:NQ]

            def out_group(i, w, ready):
                pe.wait_ge(ready, 2 * i + 2)
                e, th = i // 2, i % 2
                for t in range(4):
                    for a in range(2):
                        last = pe.matmul(PS[:, 6 + th, 128 * t:128 * t + 128], gT[:, i % 3, a, 128 * t:128 * t + 128],
                                         w[:, 2 * e + a, :], start=(a == 0), stop=(a == 1))
                last.then_inc(o_ps, 1)

            def hidden_a(i):
                e, th = i // 2, i % 2
                for a in range(2):
                    m = 2 * i + a
                    if m >= 4:
                        pe.wait_ge(h_act, m - 3)
                    pe.matmul(PS[:, m % 4, 0:448], W1[:, e, 128 * a:128 * a + 128], tokens(th),
                              start=True, stop=True).then_inc(h_ps, 1)

            for t in range(2):
                transposes(2, t)
                pe.wait_ge(ht_sb, 3 + t)
                last = pe.matmul(PS[0:16, 2 + t, :], S("wred"), HT[:, 4 * t:4 * t + 4, :], start=True, stop=True)
            last.then_inc(lg_ps, 1)
            pe.wait_ge(in_w1, 32)
            hidden_a(0)
            pe.wait_ge(lg_rd, 2)
            for t in range(NT):
                last = pe.matmul(PS[:, 5, 64 + 8 * t:72 + 8 * t], SQ[0:16, t, :], wgT[0:16, :], start=True, stop=True)
            last.then_inc(lg_ps, 1)
            for i in range(2 * NE):
                if i + 1 < 2 * NE:
                    hidden_a(i + 1)
                if i >= 2:
                    pe.wait_ge(o_add, i - 1)
                out_group(i, W2, h_act)
                if i == 3:
                    pe.wait_ge(r_max, 1)
                    pe.transpose(PS[0:64, 4, 0:128], cf.rearrange("p t e -> p (t e)"), ident).then_inc(b2_ok, 1)
                if i == 5:
                    pe.wait_ge(b2_t, 1)
                    pe.wait_ge(in_b2, 16)
                    for t in range(2):
                        last = pe.matmul(PS[:, 4 + t, :], cfT, b2d[:, 512 * t:512 * t + 512], start=True, stop=True)
                    last.then_inc(b2_ok, 1)
                if i == 11:
                    pe.wait_ge(cap_ok, 1)
                    pe.transpose(PS[0:13, 4, 0:56], sm[0:56, 576:589], C("ident")[0:56, 0:56]).then_inc(live_t, 1)
                if i == 12:
                    pe.wait_ge(live_f, 1)
                    pe.transpose(PS[0:1, 4, 64:77], sm[0:13, 592:593], C("ident")[0:13, 0:13]).then_inc(live_t, 1)

            for t in range(2):
                transposes(3, t)
                pe.wait_ge(ht_sb, 5 + t)
                pe.matmul(PS[:, 4 + t, :], S("wq"), HT[:, 4 * t:4 * t + 4, :], start=True,
                          stop=True).then_inc(q_ps, 1)
            pe.wait_ge(q_sb, 1)
            pe.wait_ge(live_ok, 1)
            live = pe.value_load(live_i[0:1, 0:1], min_val=1, max_val=NC)

            def scores(n, u):
                if first(n) and u == NT // 2:
                    pe.wait_ge(q_sb, 2)
                if u or not first(n):
                    pe.wait_ge(a_min, NT * n + u)
                for h in range(2):
                    for pr in range(2):
                        for g in range(4):
                            k = 2 * pr + h
                            last = pe.matmul(PS[0:112, g, KC * k:KC * k + KC],
                                             qbd[32 * g:32 * g + 32, 2 * u + h, 2 * pr:2 * pr + 2, :],
                                             kT[32 * g:32 * g + 32, 2 * u + h, :], start=True, stop=True,
                                             tile_position=(32 * g, 0))
                last.then_inc(a_s, 1)

            def turn(n, u):
                N = NT * n + u
                pe.wait_ge(a_os, N + 1)
                if first(n) and u == 0:
                    pe.wait_ge(x_up, 3)
                if u or not first(n):
                    pe.wait_ge(a_acc, N)
                for k in range(4):
                    last = pe.transpose(PS[0:112, 7, 128 * k:128 * k + 128], avT[:, 112 * k:112 * k + 112], ident)
                last.then_inc(a_bk, 1)

            def products(n, u):
                N = NT * n + u
                pe.wait_ge(a_pT, 4 * N + 4)
                if u or not first(n):
                    pe.wait_ge(a_os, N)
                for k in range(4):
                    for g in range(4):
                        b, pr = 2 * u + k % 2, k // 2
                        last = pe.matmul(PS[32 * g:32 * g + VW, 6, 112 * k:112 * k + 112], vC[0:KC, b, 2 * g + pr, :],
                                         pT[0:KC, u % 2, 448 * g + 112 * k:448 * g + 112 * k + 112],
                                         start=True, stop=True, tile_position=(0, 32 * g))
                last.then_inc(a_o, 1)

            def chunk(n):
                pe.wait_ge(a_v, 4 * n + 4)
                scores(n, 0)
                if first(n):
                    pe.matmul(PS[:, 6, :], C("zero")[0:1, :], C("ones")[0:1, 0:1].to_broadcast([1, 512]), start=True,
                              stop=True)
                    pe.matmul(PS[:, 7, 0:128], C("ones")[0:1, :], bo[:], start=True, stop=True).then_inc(bo_ps, 1)
                for u in range(NT):
                    N = NT * n + u
                    if u + 1 < NT:
                        scores(n, u + 1)
                    if u >= 2:
                        turn(n, u - 2)
                    if u:
                        products(n, u - 1)
                    pe.wait_ge(a_exp, N + 1)
                    for g in range(4):
                        if u or g >= 2:
                            pe.wait_ge(a_pT, 4 * N + g - 1)
                        elif not first(n):
                            pe.wait_ge(a_pT, 4 * N)
                        for k in range(4):
                            last = pe.transpose(PS[0:KC, 4 + g % 2, 112 * k:112 * k + 112],
                                                sS[0:112, u % 2, 4 * g + k, :], C("ident")[0:112, 0:112])
                        last.then_inc(a_tp, 1)
                turn(n, NT - 2)
                products(n, NT - 1)
                turn(n, NT - 1)

            chunk(0)
            with pe.If(live > 1):
                with pe.Fori(1, live) as n:
                    pe.wait_ge(a_min, NT * n)
                    project(n)
                    chunk(n)
            for b in (*range(0, NB, 2), *range(1, NB, 2)):
                if b < 2:
                    pe.wait_ge(a_fin, b + 1)
                last = pe.transpose(PS[0:64, b // 4, 112 * (b % 4):112 * (b % 4) + 112],
                                    oN[0:112, b % 2, 4 * (b // 2) * 2:4 * (b // 2) * 2 + 8, :].rearrange("p g d -> p (g d)"),
                                    C("ident")[0:112, 0:112])
            last.then_inc(a_tps, 1)
            for t in range(NT):
                if t == 0:
                    pe.wait_ge(a_oT, 2)
                if t == 4:
                    pe.wait_ge(a_oT2, 2)
                last = pe.matmul(PS[:, 4 + t // 4, 128 * (t % 4):128 * (t % 4) + 128],
                                 oT[:, 2 * t:2 * t + 2, :].rearrange("p b q -> p (b q)"), pair[:, 0:128], start=True, stop=True)
                if t % 4 == 3:
                    last.then_inc(wo_ps, 1)

            pe.wait_ge(in_w13, 32)
            for t in range(NT):
                if t % 4 == 0:
                    transposes(4, t // 4)
                    pe.wait_ge(ht_sb, 7 + t // 4)
                last = pe.matmul(PS[:, 6, 64 + 8 * t:72 + 8 * t], HT[:, t, :], S("gate"), start=True, stop=True)
            last.then_inc(lg_ps, 1)
            def hidden_b(i):
                e, th = i // 2, i % 2
                for a in range(2):
                    m = 2 * i + a
                    if m >= 3:
                        pe.wait_ge(h_mul, m - 2)
                    pe.matmul(PS[:, 2 * (m % 3), 0:448], W13[:, e, 128 * a:128 * a + 128], tokens(th),
                              start=True, stop=True)
                    pe.matmul(PS[:, 2 * (m % 3) + 1, 0:448], W13[:, e, 256 + 128 * a:384 + 128 * a], tokens(th),
                              start=True, stop=True).then_inc(h_ps, 1)

            hidden_b(0)
            for i in range(2 * NE):
                if i + 1 < 2 * NE:
                    hidden_b(i + 1)
                if i == 0:
                    pe.wait_ge(lg_cp, 2)
                pe.wait_ge(o_add, 2 * NE + max(i - 1, 0))
                out_group(i, W2B, h_mul)

        @block.scalar
        def _(act):
            act.wait_ge(in_cst, 32)
            act.activation(tg, S("g"), ACT.Tanh).then_inc(tanh_ok, 1)

            def root(n, a):
                act.wait_ge(ln_var, 2 * n - 1 + a)
                act.activation(st8[:, 3, 4 * a:4 * a + 4], st8[:, 2, 4 * a:4 * a + 4], ACT.Sqrt).then_inc(ln_std, 1)

            def copy_ht(n, a, scale):
                act.wait_ge(ht_ps, 2 * n - 1 + a)
                act.activation(HT[:, 4 * a:4 * a + 4, :], PS[:, turned_bank(n, a), :].rearrange("p (t d) -> p t d", d=128),
                               ACT.Copy, scale=scale).then_inc(ht_sb, 1)

            for b in range(NB):
                u = b // 2
                if b % 2 == 1 and u:
                    act.wait_ge(d_add, u)
                    act.activation(Dt[:, (u - 1) % 2, :], Dt[:, (u - 1) % 2, :], ACT.Sqrt).then_inc(d_root, 1)
                if b == 1:
                    root(1, 0)
                    root(1, 1)
                act.wait_ge(in_ct[b % 4], 16 * (b // 4 + 1))
                if b == 2:
                    copy_ht(1, 0, -2.0)
                    copy_ht(1, 1, -2.0)
                if b >= 2:
                    act.wait_ge(d_half, b - 1)
                act.activation(cSq[:, b % 2, :], cT[:, b % 4, :], ACT.Square).then_inc(sq_ok, 1)
            act.wait_ge(d_add, NT)
            act.activation(Dt[:, (NT - 1) % 2, :], Dt[:, (NT - 1) % 2, :], ACT.Sqrt).then_inc(d_root, 1)
            for t in range(1, SLOTS):
                if t < SLOTS - 1:
                    act.wait_ge(w_shift, t)
                    act.activation(Rv[:, t + 1, 0:1], PS[:, 0, t - 1:t],
                                   ACT.Identity, bias=C("edge")).then_inc(w_edge, 1)
                act.wait_ge(w_min, t)
                act.wait_ge(v_y, t)
                act.activation(diag[:, t % RING, :], diag[:, t % RING, :], ACT.Sign, bias=C("tiny")).then_inc(v_z, 1)
                act.wait_ge(v_z, t)
                act.activation(Rv[:, t - 1, 1:SW], diag[:, t % RING, :], ACT.Identity,
                               bias=C("ones")[:, 0:1], scale=-DIAG).then_inc(v_f, 1)
            def projected(n):
                for i in range(4):
                    act.wait_ge(a_kps, n + 1)
                    act.activation(kT[:, 4 * i:4 * i + 4, :], PS[:, i, 0:CH].rearrange("p (b k) -> p b k", b=4),
                                   ACT.Identity, bias=S("bk")).then_inc(a_kT, 1)
                for i in range(4):
                    act.wait_ge(a_vps, 4 * n + i + 1)
                    act.activation(vC[0:KC, 4 * i:4 * i + 4, :, 0:2 * DH].rearrange("p b g v -> p (b g) v"),
                                   PS[0:KC, i, :].rearrange("p (b v) -> p b v", v=2 * DH),
                                   ACT.Copy).then_inc(a_v, 1)

            act.wait_ge(pool_init, 3)
            projected(0)
            act.wait_ge(e_bc, 2)
            for c in range(NC):
                if c >= 2:
                    act.wait_ge(m_ok, c - 1)
                act.activation(G1v[:, c % 2], Ebv[:, :, 1:NQ + 1], ACT.Relu, bias=C("end")[:, c:c + 1],
                               scale=STEEP).then_inc(m_end, 1)
            act.wait_ge(wg_sq, 1)
            act.activation(wgs[0:8, 1:2], wgs[0:8, 0:1], ACT.Sqrt).then_inc(wg_std, 1)
            act.wait_ge(wg_t, 1)
            act.activation(wgT[0:16, :], PS[0:16, 3, 0:8], ACT.Copy).then_inc(lg_rd, 1)
            for a in range(2):
                root(2, a)
                copy_ht(2, a, 1.0)
            act.wait_ge(lg_ps, 1)
            act.activation(SQ[0:16, :, :], PS[0:16, 2:4, :].rearrange("p a (t d) -> p (a t) d", d=128),
                           ACT.Copy).then_inc(lg_rd, 1)
            act.wait_ge(r_exp, 1)
            act.activation(ta, lg, ACT.Exp).then_inc(r_exp, 1)
            def units(t):
                return t.rearrange("p (b q) -> p b q", q=64)[:, :, 0:NQ]

            act.wait_ge(pool_late, 1)
            for i in range(2 * NE):
                for a in range(2):
                    m = 2 * i + a
                    act.wait_ge(h_ps, m + 1)
                    if i >= 3:
                        act.wait_ge(o_ps, i - 2)
                    act.activation(units(gT[:, i % 3, a, :]), PS[:, m % 4, 0:448].rearrange("p (b q) -> p b q", q=NQ),
                                   ACT.Gelu, bias=S("b1")[:, 2 * (i // 2) + a:2 * (i // 2) + a + 1]).then_inc(h_act, 1)
                if i == 4:
                    act.wait_ge(b2_ok, 1)
                    act.activation(cfT, PS[0:64, 4, 0:128], ACT.Copy).then_inc(b2_t, 1)
            for a in range(2):
                root(3, a)
                copy_ht(3, a, 1.0)
            act.wait_ge(live_ok, 1)
            live = act.value_load(live_i[0:1, 0:1], min_val=1, max_val=NC)

            def copy_products(n, u):
                N = NT * n + u
                act.wait_ge(a_o, N + 1)
                if u or not first(n):
                    act.wait_ge(a_bk, N)
                act.activation(avT, PS[:, 6, 0:448], ACT.Copy).then_inc(a_os, 1)

            def chunk(n):
                for u in range(NT):
                    N = NT * n + u
                    act.wait_ge(a_sub, N + 1)
                    act.activation(sS[0:112, u % 2], sS[0:112, u % 2], ACT.Exp).then_inc(a_exp, 1)
                    act.wait_ge(a_max, 3 * N + 3)
                    if u > 3 or not first(n):
                        act.wait_ge(a_am, N - 3)
                    act.activation(alpha[0:112, u % 4], drop[0:112, u % 2], ACT.Exp).then_inc(a_al, 1)
                    for g in range(4):
                        act.wait_ge(a_tp, 4 * N + g + 1)
                        if u > 1 or not first(n):
                            act.wait_ge(a_o, N - 1)
                        act.activation(pT[0:KC, u % 2, 448 * g:448 * g + 448],
                                       PS[0:KC, 4 + g % 2, 0:448], ACT.Copy).then_inc(a_pT, 1)
                    if u:
                        copy_products(n, u - 1)
                copy_products(n, NT - 1)

            chunk(0)
            with act.If(live > 1):
                with act.Fori(1, live) as n:
                    projected(n)
                    chunk(n)
            act.wait_ge(a_tps, 1)
            for h in range(2):
                act.activation(outputs_T(0, h), outputs(0, h), ACT.Identity,
                               bias=pair[0:64, 128 + h:129 + h]).then_inc(a_oT, 1)
            for a in range(2):
                root(4, a)
                copy_ht(4, a, 1.0)
            act.wait_ge(r_exp, 3)
            act.activation(ta, lg, ACT.Exp).then_inc(r_exp, 1)
            for m in range(4 * NE):
                act.wait_ge(h_ps, 4 * NE + m + 1)
                if m >= 2:
                    act.wait_ge(h_mul, m - 1)
                act.activation(sil[:, m % 2, 0:448], PS[:, 2 * (m % 3), 0:448], ACT.Silu).then_inc(h_act, 1)

        @block.vector
        def _(dve):
            n_vec = [0]

            def link(ins):
                n_vec[0] += 1
                ins.then_inc(vec, 1)
                dve.wait_ge(vec, n_vec[0])

            s8 = [st8[:, i, :] for i in range(6)]

            def layernorm(n, a):
                half = range(4 * a, 4 * a + 4)
                for t in half:
                    last = dve.bn_stats(bnst[:, t, :], X[:, t, :])
                link(last)
                for t in half:
                    last = dve.bn_aggr(mv[:, t, :], bnst[:, t, :])
                link(last)
                dve.tensor_scalar(s8[2][:, 4 * a:4 * a + 4], mv[:, 4 * a:4 * a + 4, 1], EPS, None, ALU.add).then_inc(ln_var, 1)
                dve.wait_ge(ln_std, 2 * n - 1 + a)
                link(dve.reciprocal(s8[4][:, 4 * a:4 * a + 4], s8[3][:, 4 * a:4 * a + 4]))
                for t in half:
                    last = dve.tensor_scalar(H[:, t, :], X[:, t, :], mv[:, t, 0:1], s8[4][:, t:t + 1],
                                             ALU.subtract, ALU.mult)
                last.then_inc(ln_out, 1)

            dve.wait_ge(in_cst, 32)
            dve.wait_ge(in_x, 32)
            dve.wait_ge(pool_init, 1)
            layernorm(1, 0)
            layernorm(1, 1)
            dve.wait_ge(ln_out, 2)
            link(dve.tensor_tensor(SQ, H, H, ALU.mult))
            link(dve.tensor_reduce(s8[5], SQ, AX, ALU.add))
            dve.wait_ge(pool_init, 2)
            dve.tensor_copy(Rv[:, 0, :], C("first")).then_inc(w_row, 1)
            for u in range(NT):
                dve.wait_ge(d_half, 2 * u + 2)
                if u >= 2:
                    dve.wait_ge(d_put[u % 2][0], 16 * sum(map(len, by_sync[u % 2:u:2])))
                    dve.wait_ge(d_put[u % 2][1], 16 * sum(map(len, by_pool[u % 2:u:2])))
                dve.tensor_scalar(Dt[:, u % 2, :].rearrange("p (i k) -> p i k", i=3),
                                  PS[:, 3 * (u % 2):3 * (u % 2) + 3, 0:CH], s8[5][:, u:u + 1], 0.0,
                                  ALU.add, ALU.max).then_inc(d_add, 1)
            for i in range(2):
                dve.wait_ge(d_put[i][0], 16 * sum(map(len, by_sync[i::2])))
                dve.wait_ge(d_put[i][1], 16 * sum(map(len, by_pool[i::2])))

            def tie(s):
                dve.wait_ge(v_x, s)
                dve.wait_ge(v_z, s)
                dve.scalar_tensor_tensor(over[:, s % RING, :], diag[:, s % RING, :], TINY, over[:, s % RING, :],
                                         ALU.mult, ALU.add).then_inc(v_q, 1)

            def choice(s):
                dve.wait_ge(v_q, s)
                dve.wait_ge(v_f, s)
                dve.scalar_tensor_tensor(Rv[:, s - 1, 1:SW], over[:, s % RING, :], 0.0, Rv[:, s - 1, 1:SW],
                                         ALU.is_gt, ALU.mult).then_inc(v_u, 1)

            for t in range(1, SLOTS):
                if t > 1:
                    dve.wait_ge(w_row, t)
                dve.tensor_tensor(best[:, t % RING, :], Rv[:, t - 1, 1:SW], Rv[:, t - 1, 0:BR], ALU.min).then_inc(w_min, 1)
                if t > 2:
                    tie(t - 2)
                dve.wait_ge(w_min, t)
                if t > 1:
                    dve.wait_ge(w_edge, t - 1)
                dve.tensor_tensor_scan(Rv[:, t, 1:SW], best[:, t % RING, :], Rv[:, t, 1:SW], Rv[:, t, 0:1],
                                       ALU.min, ALU.add).then_inc(w_row, 1)
                if t > 2:
                    choice(t - 2)
            for t in range(SLOTS - 2, SLOTS):
                tie(t)
                choice(t)
            dve.wait_ge(v_put, 16 * puts)

            dve.memset(E[:, 0:1], 0.0)
            link(dve.memset(E[:, NQ:NQ + 1], float(NK - 1)))
            for n in range(NQ - 1):
                if n:
                    dve.wait_ge(b_e, n)
                dve.scalar_tensor_tensor(leaving[:], C("rows"), E[:, NQ - n:NQ - n + 1], C("rows"), ALU.is_le, ALU.mult).then_inc(b_g, 1)
                dve.wait_ge(b_g, n + 1)
                dve.tensor_tensor_reduce(leaving[:], leaving[:], Vcol[:, NQ - 1 - n, :],
                                         1.0, 0.0, ALU.mult, ALU.max, block_max[:]).then_inc(b_max, 1)
                dve.wait_ge(b_max, n + 1)
                dve.transpose(blocks[:], block_max[:].to_broadcast([128, 32])).then_inc(b_t, 1)
                dve.wait_ge(b_t, n + 1)
                dve.tensor_tensor_reduce(blocks[:], blocks[:], C("same"), 1.0, 0.0, ALU.mult, ALU.max,
                                         E[:, NQ - 1 - n:NQ - n]).then_inc(b_e, 1)
            dve.wait_ge(b_e, NQ - 1)
            dve.wait_ge(a_vps, 4)
            dve.tensor_tensor(Ed.rearrange("p (b j) -> p b j", b=NB),
                              E[:, None, :].to_broadcast([128, NB, NQ + 1]),
                              C("own")[:, :, None].to_broadcast([128, NB, NQ + 1]), ALU.mult).then_inc(e_tab, 1)
            dve.wait_ge(e_bc, 1)
            W = NB * (NQ + 1) // 2
            dve.tensor_copy(Eb[:].rearrange("p (i w) -> p i w", i=2), PS[:, 3:5, 0:W]).then_inc(e_bc, 1)
            dve.wait_ge(e_bc, 2)
            for c in range(NC):
                dve.wait_ge(m_end, c + 1)
                dve.scalar_tensor_tensor(Mk[:, c], Ebv[:, :, 0:NQ], C("keyh")[:, c:c + 1], G1v[:, c % 2], ALU.is_le,
                                         ALU.min).then_inc(m_ok, 1)
            dve.wait_ge(tanh_ok, 1)
            dve.wait_ge(in_w, 48)
            link(dve.tensor_tensor(wgn[0:8, :], wg_s[:], wg_s[:], ALU.mult))
            dve.tensor_reduce(wgs[0:8, 0:1], wgn[0:8, :], AX, ALU.add).then_inc(wg_sq, 1)
            dve.wait_ge(wg_std, 1)
            link(dve.tensor_scalar(wgs[0:8, 2:3], wgs[0:8, 1:2], 1e-4, None, ALU.max))
            link(dve.reciprocal(wgs[0:8, 3:4], wgs[0:8, 2:3]))
            dve.tensor_scalar(wgn[0:8, :], wg_s[:], wgs[0:8, 3:4], None, ALU.mult).then_inc(wg_r, 1)
            def add_half(a, ready, n, bank, gate, count):
                dve.wait_ge(ready, n)
                dve.scalar_tensor_tensor(Xh[:, a, :], PS[:, bank, :], gate, Xh[:, a, :], ALU.mult, ALU.add).then_inc(x_up, 1)
                dve.wait_ge(x_up, count)

            Xh = X[:].rearrange("p t d -> p (t d)").rearrange("p (a w) -> p a w", a=2)
            for a in range(2):
                add_half(a, x_ps, a + 1, 5 + a, tg[:, 0:1], a + 1)
                layernorm(2, a)

            def softmax(n):
                dve.tensor_copy(lg, PS[:, 5 if n == 2 else 6, 64:128].rearrange("p (t e) -> p t e", t=NT)).then_inc(lg_cp, 1)
                dve.wait_ge(lg_cp, n // 2)
                link(dve.tensor_reduce(s8[0], lg, AX, ALU.max))
                dve.tensor_tensor(lg, lg, s8[0][:, :, None].to_broadcast([128, NT, NE]), ALU.subtract).then_inc(r_exp, 1)
                dve.wait_ge(r_exp, n)
                link(dve.tensor_reduce(s8[0], ta, AX, ALU.add))
                link(dve.reciprocal(s8[1], s8[0]))
                link(dve.tensor_tensor(ta, ta, s8[1][:, :, None].to_broadcast([128, NT, NE]), ALU.mult))

            def first_of(dst, src, w, m):
                tmp = td[:, :, 0:w]
                rank = C("rank8" if w == 8 else "rank4")[:, None, 0:w].to_broadcast([128, NT, w])
                link(dve.tensor_reduce(m, src, AX, ALU.max))
                link(dve.tensor_tensor(dst, src, m[:, :, None].to_broadcast([128, NT, w]), ALU.is_equal))
                link(dve.tensor_tensor(dst, dst, rank, ALU.mult))
                link(dve.tensor_reduce(s8[5], dst, AX, ALU.max))
                link(dve.tensor_tensor(dst, dst, s8[5][:, :, None].to_broadcast([128, NT, w]), ALU.is_equal))

            def experts_add(base, i):
                e, th = i // 2, i % 2
                dve.wait_ge(o_ps, base + i + 1)
                for t in range(4):
                    ins = dve.scalar_tensor_tensor(X[:, 4 * th + t, :], PS[:, 6 + th, 128 * t:128 * t + 128],
                                                   cf[:, 4 * th + t, e:e + 1], X[:, 4 * th + t, :], ALU.mult, ALU.add)
                ins.then_inc(o_add, 1)
                dve.wait_ge(o_add, base + i + 1)

            Xh = X[:].rearrange("p t d -> p (t d)").rearrange("p (a w) -> p a w", a=2)

            dve.wait_ge(lg_ps, 2)
            softmax(2)
            first_of(cf, ta, NE, s8[2])
            link(dve.tensor_tensor(cf, cf, s8[2][:, :, None].to_broadcast([128, NT, NE]), ALU.mult))
            dve.tensor_scalar(cf, cf, tg[:, 2:3], None, ALU.mult).then_inc(r_max, 1)
            dve.wait_ge(r_max, 1)
            for i in range(2 * NE):
                if i == 2 * NE - 1:
                    layernorm(3, 0)
                experts_add(0, i)
                if i == 7:
                    dve.wait_ge(b2_ok, 2)
                    link(dve.tensor_tensor(Xh, Xh, PS[:, 4:6, :], ALU.add))
                if i == 7:
                    dve.wait_ge(in_mask, 32)
                    link(dve.tensor_copy(capA[0:112], msk8[0:112]))
                if i == 8:
                    link(dve.tensor_scalar(capB[0:112], capA[0:112], 0.5, None, ALU.is_lt))
                    link(dve.tensor_reduce(sm[0:56, 576:588], capB[0:56].rearrange("p (c k) -> p c k", c=NC), AX, ALU.max))
                if i == 9:
                    link(dve.tensor_reduce(sm[0:56, 588:589], sm[0:56, 576:588], AX, ALU.max))
                    link(dve.tensor_scalar(sm[0:56, 588:589], sm[0:56, 588:589], 0.5, None, ALU.is_lt))
                    link(dve.tensor_scalar(capA[0:112], capA[0:112], -1e9, None, ALU.mult))
                if i == 10:
                    dve.scalar_tensor_tensor(cap[0:112], capB[0:112], MAXV, capA[0:112], ALU.mult, ALU.add).then_inc(cap_ok, 1)
                if i == 11:
                    dve.wait_ge(cap_ok, 1)
                    dve.wait_ge(live_t, 1)
                    dve.tensor_reduce(sm[0:13, 592:593], PS[0:13, 4, 0:56], AX, ALU.max).then_inc(live_f, 1)
                if i == 12:
                    dve.wait_ge(live_t, 2)
                    link(dve.tensor_tensor(sm[0:1, 596:609], PS[0:1, 4, 64:77], C("late")[0:1, 0:13], ALU.mult))
                    link(dve.tensor_reduce(sm[0:1, 612:613], sm[0:1, 596:609], AX, ALU.max))
                    dve.tensor_copy(live_i[0:1, 0:1], sm[0:1, 612:613]).then_inc(live_ok, 1)

            layernorm(3, 1)
            for i in range(2):
                dve.wait_ge(q_ps, i + 1)
                q = PS[:, 4 + i, :].rearrange("p (b q) -> p b q", b=8)[:, :, 0:NQ]
                for h in range(4):
                    last = dve.tensor_scalar(qbd[:, 8 * i:8 * i + 8, h, :], q, S("bq"), C("sel")[:, h:h + 1],
                                             ALU.add, ALU.mult)
                last.then_inc(q_sb, 1)
            live = dve.value_load(live_i[0:1, 0:1], min_val=1, max_val=NC)

            def accumulate(n, u):
                N = NT * n + u
                a = acc[0:112, u]
                dve.wait_ge(a_al, N + 1)
                if u or not first(n):
                    dve.wait_ge(a_acc, N)
                dve.tensor_tensor(a, a, alpha[0:112, u % 4, :, None].to_broadcast([112, 16, VW]), ALU.mult).then_inc(a_am, 1)
                dve.wait_ge(a_am, N + 1)
                dve.wait_ge(a_bk, N + 1)
                a = a.rearrange("p (g k) v -> p g k v", k=4)
                dve.tensor_tensor(a, a, PS[0:112, 7, :].rearrange("p (k g v) -> p g k v", k=4, g=4)[:, :, :, 0:VW],
                                  ALU.add).then_inc(a_acc, 1)

            def chunk(n):
                key = (NC - 1) * KC if first(n) else dve.snap(n * -KC + (NC - 1) * KC)
                k = cap[0:112, bass.ds(key, KC)]
                for u in range(NT):
                    N = NT * n + u
                    S2 = sS[0:112, u % 2]
                    dve.wait_ge(a_s, N + 1)
                    if u > 1 or not first(n):
                        dve.wait_ge(a_tp, 4 * N - 4)
                    dve.tensor_tensor(S2.rearrange("p (g r) k -> p g r k", g=4),
                                      PS[0:112, 0:4, 0:CH].rearrange("p g (r k) -> p g r k", k=KC),
                                      k[:, None, None, :].to_broadcast([112, 4, 4, KC]), ALU.min).then_inc(a_min, 1)
                    dve.wait_ge(a_min, N + 1)
                    dve.tensor_reduce(mtmp[0:112, u % 2], S2, AX, ALU.max).then_inc(a_max, 1)
                    dve.wait_ge(a_max, 3 * N + 1)
                    if u > 1 or not first(n):
                        dve.wait_ge(a_mr, N - 1)
                    dve.tensor_tensor(mnew[0:112, u % 2], mtmp[0:112, u % 2], mrun[0:112, u], ALU.max).then_inc(a_max, 1)
                    dve.wait_ge(a_max, 3 * N + 2)
                    if u > 1 or not first(n):
                        dve.wait_ge(a_al, N - 1)
                    dve.tensor_tensor(drop[0:112, u % 2], mrun[0:112, u], mnew[0:112, u % 2], ALU.subtract).then_inc(a_max, 1)
                    if first(n) and u == 0:
                        dve.wait_ge(bo_ps, 1)
                        dve.scalar_tensor_tensor(X[:], PS[:, 7:8, 0:128].to_broadcast([128, NT, 128]), tg[:, 1:2], X[:],
                                             ALU.mult, ALU.add).then_inc(x_up, 1)
                    if u > 1:
                        accumulate(n, u - 2)
                accumulate(n, NT - 2)
                accumulate(n, NT - 1)

            chunk(0)
            with dve.If(live > 1):
                with dve.Fori(1, live) as n:
                    chunk(n)
            dve.wait_ge(a_acc, live * NT)
            dve.wait_ge(a_mr, live * NT)
            link(dve.reciprocal(mrun[0:112], acc[0:112, :, :, VW - 1]))
            a = acc[0:112].rearrange("p u (g h) v -> p (u g) h v", h=2)
            rc = mrun[0:112].rearrange("p u (g h) -> p (u g) h", h=2)
            for h in range(2):
                o = oN[0:112, h]
                link(dve.tensor_scalar(o, a[:, :, h, 0:DH], C("half")[0:112, 0:1], None, ALU.mult))
                link(dve.scalar_tensor_tensor(o, a[:, :, h, DH:2 * DH], C("half")[0:112, 1:2], o, ALU.mult, ALU.add))
                dve.tensor_tensor(o, o, rc[:, :, h, None].to_broadcast([112, 64, DH]), ALU.mult).then_inc(a_fin, 1)
            def gate_units(m):
                i, a = m // 2, m % 2
                dve.wait_ge(h_act, 4 * NE + m + 1)
                if i >= 3:
                    dve.wait_ge(o_ps, 2 * NE + i - 2)
                dve.tensor_tensor(gT[:, i % 3, a, :].rearrange("p (b q) -> p b q", q=64)[:, :, 0:NQ],
                                  sil[:, m % 2, 0:448].rearrange("p (b q) -> p b q", q=NQ),
                                  PS[:, 2 * (m % 3) + 1, 0:448].rearrange("p (b q) -> p b q", q=NQ), ALU.mult).then_inc(h_mul, 1)

            dve.wait_ge(a_tps, 1)
            for h in range(2):
                dve.tensor_scalar(outputs_T(1, h), outputs(1, h), pair[0:64, 128 + h:129 + h], None,
                                  ALU.add).then_inc(a_oT2, 1)
            for a in range(2):
                add_half(a, wo_ps, a + 1, 4 + a, tg[:, 1:2], 4 + a)
                layernorm(4, a)
            dve.wait_ge(lg_ps, 3)
            softmax(4)
            gate_units(0)
            gate_units(1)
            grp, oh = tb[:, :, 0:4], tc[:, :, 0:4]
            twos = ta.rearrange("p t (g i) -> p t g i", i=2)
            link(dve.tensor_tensor(grp, twos[:, :, :, 0], twos[:, :, :, 1], ALU.max))
            first_of(oh, grp, 4, s8[2])
            link(dve.scalar_tensor_tensor(grp, oh, -2.0, grp, ALU.mult, ALU.add))
            o2 = tb[:, :, 4:8]
            first_of(o2, grp, 4, s8[2])
            link(dve.tensor_tensor(oh, oh, o2, ALU.add))
            gate_units(2)
            gate_units(3)
            link(dve.tensor_tensor(twos, twos, oh[:, :, :, None].to_broadcast([128, NT, 4, 2]), ALU.mult))
            first_of(tb, ta, NE, s8[2])
            link(dve.scalar_tensor_tensor(cf, tb, -2.0, ta, ALU.mult, ALU.add))
            first_of(tc, cf, NE, s8[3])
            link(dve.tensor_tensor(s8[2], s8[2], s8[3], ALU.add))
            link(dve.reciprocal(s8[3], s8[2]))
            link(dve.tensor_tensor(tb, tb, tc, ALU.add))
            link(dve.tensor_tensor(cf, tb, ta, ALU.mult))
            link(dve.tensor_tensor(cf, cf, s8[3][:, :, None].to_broadcast([128, NT, NE]), ALU.mult))
            dve.tensor_scalar(cf, cf, tg[:, 3:4], None, ALU.mult).then_inc(r_max, 1)
            dve.wait_ge(r_max, 2)
            for m in range(2, 4 * NE):
                i, a = m // 2, m % 2
                if m >= 4:
                    gate_units(m)
                if a and i:
                    experts_add(2 * NE, i - 1)
            experts_add(2 * NE, 2 * NE - 1)


def kernel(**inputs):
    import concourse.bacc as _bacc
    from concourse.bass_utils import run_bass_kernel_spmd as _run

    a = {k: np.asarray(v) for k, v in inputs.items()}
    ctx = np.ascontiguousarray(a["ctx_1024"])
    parts = {"wq": a["L1_xattn_W_q"], "wk": a["L1_xattn_W_k"], "wv": a["L1_xattn_W_v"],
             "wred": a["L0_ffn_w_red"], "gate": a["L1_ffn_gate_w"].T, "bq": a["L1_xattn_b_q"][:, None],
             "bk": a["L1_xattn_b_k"][:, None],
             "b1": a["L0_ffn_b1"].reshape(2 * NE, 128).T,
             "g": np.broadcast_to(np.concatenate([a["g_xattn"], a["g_ffn"]])[None, :], (128, 4))}
    b2 = np.zeros((NT, NE, NT, 128), np.float32)
    for t in range(NT):
        b2[t, :, t] = a["L0_ffn_b2"]
    b2 = b2.reshape(NT * NE, NT * 128)
    arrays = {
        "x": a["x"],
        "ctx": ctx,
        "ctxT": ctx.transpose(0, 2, 1),
        "mask": a["mask_1x1xSxS2_bk1"].reshape(NQ, NK),
        "cst": const_values(),
        "small": np.concatenate([parts[n] for n, _ in SMALL], axis=1),
        "bo": a["L1_xattn_b_o"][None, :],
        "wg": a["L0_ffn_wg"],
        "pair": np.concatenate([a["L1_xattn_W_o"].reshape(8, 2, DH, 128).transpose(1, 0, 2, 3).reshape(128, 128),
                                np.tile(a["L1_xattn_b_v"].reshape(8, 2, DH).transpose(0, 2, 1).reshape(64, 2), (2, 1))],
                               axis=1),
        "b2": b2,
        "w1": a["L0_ffn_W1"],
        "w2": a["L0_ffn_W2"].reshape(2 * NE, 128, 128).transpose(1, 0, 2),
        "w13": a["L1_ffn_w13_weight"].transpose(2, 0, 1),
        "w2b": a["L1_ffn_w2_weight"].transpose(0, 2, 1).reshape(2 * NE, 128, 128).transpose(1, 0, 2),
    }
    nc = _bacc.Bacc("TRN2", target_bir_lowering=False, num_devices=1)
    fed, args = {}, []
    for name, v in arrays.items():
        v = np.ascontiguousarray(v)
        fed[f"in_{name}"] = v
        args.append(nc.dram_tensor(f"in_{name}", v.shape, mybir.dt.from_np(v.dtype), kind="ExternalInput").ap())
    out = nc.dram_tensor("out_0", (NB, NQ, ND), F32, kind="ExternalOutput").ap()
    flamingo(nc, *args, out)
    r = _run(nc, [fed], core_ids=[0])
    return r.results[0]["out_0"]
```
